# Optimizing a Trainium2 kernel written in Bass

```python
import numpy as np
import jax
import jax.numpy as jnp

def _softmax(x, axis=-1):
    return jax.nn.softmax(x, axis=axis)

def _gelu(x):
    return jax.nn.gelu(x, approximate=True)

def _silu(x):
    return jax.nn.silu(x)

def _sigmoid(x):
    return jax.nn.sigmoid(x)

def _layernorm(x, axis=-1, eps=1e-05):
    m = jnp.mean(x, axis=axis, keepdims=True)
    v = jnp.var(x, axis=axis, keepdims=True)
    return (x - m) / jnp.sqrt(v + eps)

def _scatter_add(tgt, idx, src, axis=0):
    return tgt.at[idx].add(src)

def _segment_sum(src, seg, n):
    return jax.ops.segment_sum(src, seg, n)
kernel_name = 'mk_gnn_ffn_d1_gnn_r16_0338d9'

def setup_inputs(seed: int=0):
    np.random.seed(seed)
    _w = jnp.asarray

    def _rec_inputs():
        import jax
        import jax.numpy as jnp
        _gk = jax.random.key(seed)
        x = -0.000364 + 1 * jax.random.normal(jax.random.fold_in(_gk, 1), (625, 768), jnp.float32)
        src = jax.random.randint(jax.random.fold_in(_gk, 2), (20000,), 0, 625, jnp.int32)
        dst = jax.random.randint(jax.random.fold_in(_gk, 3), (20000,), 0, 625, jnp.int32)
        _o = jnp.argsort(dst, stable=True)
        src = src[_o]
        dst = dst[_o]
        return (x, src, dst)
    x, src, dst = _rec_inputs()

    def _L0_gnn_setup():
        import jax, jax.numpy as jnp
        import numpy as np
        N_NODES = 1250
        N_EDGES = 10000
        IN_DIM = 768
        HID = 256
        HEADS = 4
        OUT_DIM = 768
        LN_EPS = 1e-05

        def _add_self_loops(edge_index, n):
            loop = jnp.arange(n, dtype=edge_index.dtype)
            return jnp.concatenate([edge_index, jnp.stack([loop, loop])], axis=1)

        def gat_conv(x, edge_index, W, a_src, a_dst, bias, heads, out_ch, concat):
            n = x.shape[0]
            ei = _add_self_loops(edge_index, n)
            src, dst = (ei[0], ei[1])
            xl = (x @ W).reshape(n, heads, out_ch)
            alpha_src = jnp.einsum('nhc,hc->nh', xl, a_src)
            alpha_dst = jnp.einsum('nhc,hc->nh', xl, a_dst)
            e = jax.nn.leaky_relu(alpha_src[src] + alpha_dst[dst], 0.2)
            m = jax.ops.segment_max(e, dst, num_segments=n)
            e = jnp.exp(e - m[dst])
            s = jax.ops.segment_sum(e, dst, num_segments=n)
            alpha = e / (s[dst] + 1e-16)
            msg = xl[src] * alpha[:, :, None]
            out = jax.ops.segment_sum(msg, dst, num_segments=n)
            out = out.reshape(n, heads * out_ch) if concat else out.mean(axis=1)
            return out + bias

        def layer_norm(x, g, b):
            mu = jnp.mean(x, axis=-1, keepdims=True)
            var = jnp.var(x, axis=-1, keepdims=True)
            return (x - mu) * jax.lax.rsqrt(var + LN_EPS) * g + b
        key = jax.random.key(seed)
        ks = jax.random.split(key, 16)
        s = 0.02
        HC = HID * HEADS
        return {'x': jax.random.normal(ks[0], (N_NODES, IN_DIM), jnp.float32), 'edge_index': jax.random.randint(ks[1], (2, N_EDGES), 0, N_NODES, jnp.int64 if jax.config.jax_enable_x64 else jnp.int32), 'W1': jax.random.normal(ks[2], (IN_DIM, HC), jnp.float32) * s, 'a_src1': jax.random.normal(ks[3], (HEADS, HID), jnp.float32) * s, 'a_dst1': jax.random.normal(ks[4], (HEADS, HID), jnp.float32) * s, 'b1': jnp.zeros((HC,), jnp.float32), 'g1': jnp.ones((HC,), jnp.float32), 'be1': jnp.zeros((HC,), jnp.float32), 'Wr1': jax.random.normal(ks[5], (IN_DIM, HC), jnp.float32) * s, 'br1': jnp.zeros((HC,), jnp.float32), 'W2': jax.random.normal(ks[6], (HC, OUT_DIM), jnp.float32) * s, 'a_src2': jax.random.normal(ks[7], (1, OUT_DIM), jnp.float32) * s, 'a_dst2': jax.random.normal(ks[8], (1, OUT_DIM), jnp.float32) * s, 'b2': jnp.zeros((OUT_DIM,), jnp.float32), 'g2': jnp.ones((OUT_DIM,), jnp.float32), 'be2': jnp.zeros((OUT_DIM,), jnp.float32), 'Wr2': jax.random.normal(ks[9], (HC, OUT_DIM), jnp.float32) * s, 'br2': jnp.zeros((OUT_DIM,), jnp.float32)}
    _L0_gnn_all = _L0_gnn_setup()
    _L0_gnn_in = {k: v for k, v in _L0_gnn_all.items() if k in ('W1', 'a_src1', 'a_dst1', 'b1', 'g1', 'be1', 'Wr1', 'br1', 'W2', 'a_src2', 'a_dst2', 'b2', 'g2', 'be2', 'Wr2', 'br2')}
    del _L0_gnn_all

    def _L0_ffn_setup():
        import jax, jax.numpy as jnp
        import numpy as np
        B, T, D = (2, 1024, 768)
        H, HS = (12, 64)
        E, K = (8, 1)
        DF = 4 * D
        EPS = 1e-05

        def _ln(x, g, b):
            mu = jnp.mean(x, axis=-1, keepdims=True)
            var = jnp.mean(jnp.square(x - mu), axis=-1, keepdims=True)
            return (x - mu) * jax.lax.rsqrt(var + EPS) * g + b
        key = jax.random.key(seed)
        ks = jax.random.split(key, 12)
        s = 0.02
        return {'x': jax.random.normal(ks[0], (B, T, D), dtype=jnp.float32), 'ln1_g': jnp.ones((D,), jnp.float32), 'ln1_b': jnp.zeros((D,), jnp.float32), 'ln2_g': jnp.ones((D,), jnp.float32), 'ln2_b': jnp.zeros((D,), jnp.float32), 'Wq': jax.random.normal(ks[1], (H, D, HS), jnp.float32) * s, 'Wk': jax.random.normal(ks[2], (H, D, HS), jnp.float32) * s, 'Wv': jax.random.normal(ks[3], (H, D, HS), jnp.float32) * s, 'Wp': jax.random.normal(ks[4], (D, D), jnp.float32) * s, 'bp': jnp.zeros((D,), jnp.float32), 'Wg': jax.random.normal(ks[5], (D, E), jnp.float32) * s, 'W1': jax.random.normal(ks[6], (E, D, DF), jnp.float32) * s, 'b1': jnp.zeros((E, DF), jnp.float32), 'W2': jax.random.normal(ks[7], (E, DF, D), jnp.float32) * s, 'b2': jnp.zeros((E, D), jnp.float32)}
    _L0_ffn_all = _L0_ffn_setup()
    _L0_ffn_in = {k: v for k, v in _L0_ffn_all.items() if k in ('ln1_g', 'ln1_b', 'ln2_g', 'ln2_b', 'Wq', 'Wk', 'Wv', 'Wp', 'bp', 'Wg', 'W1', 'b1', 'W2', 'b2')}
    del _L0_ffn_all
    return {'x': x, 'src': src, 'dst': dst, 'L0_gnn_W1': _L0_gnn_in['W1'], 'L0_gnn_a_src1': _L0_gnn_in['a_src1'], 'L0_gnn_a_dst1': _L0_gnn_in['a_dst1'], 'L0_gnn_b1': _L0_gnn_in['b1'], 'L0_gnn_g1': _L0_gnn_in['g1'], 'L0_gnn_be1': _L0_gnn_in['be1'], 'L0_gnn_Wr1': _L0_gnn_in['Wr1'], 'L0_gnn_br1': _L0_gnn_in['br1'], 'L0_gnn_W2': _L0_gnn_in['W2'], 'L0_gnn_a_src2': _L0_gnn_in['a_src2'], 'L0_gnn_a_dst2': _L0_gnn_in['a_dst2'], 'L0_gnn_b2': _L0_gnn_in['b2'], 'L0_gnn_g2': _L0_gnn_in['g2'], 'L0_gnn_be2': _L0_gnn_in['be2'], 'L0_gnn_Wr2': _L0_gnn_in['Wr2'], 'L0_gnn_br2': _L0_gnn_in['br2'], 'L0_ffn_ln1_g': _L0_ffn_in['ln1_g'], 'L0_ffn_ln1_b': _L0_ffn_in['ln1_b'], 'L0_ffn_ln2_g': _L0_ffn_in['ln2_g'], 'L0_ffn_ln2_b': _L0_ffn_in['ln2_b'], 'L0_ffn_Wq': _L0_ffn_in['Wq'], 'L0_ffn_Wk': _L0_ffn_in['Wk'], 'L0_ffn_Wv': _L0_ffn_in['Wv'], 'L0_ffn_Wp': _L0_ffn_in['Wp'], 'L0_ffn_bp': _L0_ffn_in['bp'], 'L0_ffn_Wg': _L0_ffn_in['Wg'], 'L0_ffn_W1': _L0_ffn_in['W1'], 'L0_ffn_b1': _L0_ffn_in['b1'], 'L0_ffn_W2': _L0_ffn_in['W2'], 'L0_ffn_b2': _L0_ffn_in['b2']}

def reference(x, src, dst, L0_gnn_W1, L0_gnn_a_src1, L0_gnn_a_dst1, L0_gnn_b1, L0_gnn_g1, L0_gnn_be1, L0_gnn_Wr1, L0_gnn_br1, L0_gnn_W2, L0_gnn_a_src2, L0_gnn_a_dst2, L0_gnn_b2, L0_gnn_g2, L0_gnn_be2, L0_gnn_Wr2, L0_gnn_br2, L0_ffn_ln1_g, L0_ffn_ln1_b, L0_ffn_ln2_g, L0_ffn_ln2_b, L0_ffn_Wq, L0_ffn_Wk, L0_ffn_Wv, L0_ffn_Wp, L0_ffn_bp, L0_ffn_Wg, L0_ffn_W1, L0_ffn_b1, L0_ffn_W2, L0_ffn_b2):
    import jax
    import jax.numpy as jnp

    def _L0_gnn_ref(x, edge_index, W1, a_src1, a_dst1, b1, g1, be1, Wr1, br1, W2, a_src2, a_dst2, b2, g2, be2, Wr2, br2):
        import jax, jax.numpy as jnp
        import numpy as np
        N_NODES = 1250
        N_EDGES = 10000
        IN_DIM = 768
        HID = 256
        HEADS = 4
        OUT_DIM = 768
        LN_EPS = 1e-05

        def _add_self_loops(edge_index, n):
            loop = jnp.arange(n, dtype=edge_index.dtype)
            return jnp.concatenate([edge_index, jnp.stack([loop, loop])], axis=1)

        def gat_conv(x, edge_index, W, a_src, a_dst, bias, heads, out_ch, concat):
            n = x.shape[0]
            ei = _add_self_loops(edge_index, n)
            src, dst = (ei[0], ei[1])
            xl = (x @ W).reshape(n, heads, out_ch)
            alpha_src = jnp.einsum('nhc,hc->nh', xl, a_src)
            alpha_dst = jnp.einsum('nhc,hc->nh', xl, a_dst)
            e = jax.nn.leaky_relu(alpha_src[src] + alpha_dst[dst], 0.2)
            m = jax.ops.segment_max(e, dst, num_segments=n)
            e = jnp.exp(e - m[dst])
            s = jax.ops.segment_sum(e, dst, num_segments=n)
            alpha = e / (s[dst] + 1e-16)
            msg = xl[src] * alpha[:, :, None]
            out = jax.ops.segment_sum(msg, dst, num_segments=n)
            out = out.reshape(n, heads * out_ch) if concat else out.mean(axis=1)
            return out + bias

        def layer_norm(x, g, b):
            mu = jnp.mean(x, axis=-1, keepdims=True)
            var = jnp.var(x, axis=-1, keepdims=True)
            return (x - mu) * jax.lax.rsqrt(var + LN_EPS) * g + b
        h0 = x
        h = gat_conv(x, edge_index, W1, a_src1, a_dst1, b1, HEADS, HID, True)
        h = layer_norm(h, g1, be1)
        h = jax.nn.relu(h)
        h = h + (h0 @ Wr1 + br1)
        h1 = h
        h = gat_conv(h, edge_index, W2, a_src2, a_dst2, b2, 1, OUT_DIM, False)
        h = layer_norm(h, g2, be2)
        h = h + (h1 @ Wr2 + br2)
        return h

    def _L0_ffn_ref(x, ln1_g, ln1_b, ln2_g, ln2_b, Wq, Wk, Wv, Wp, bp, Wg, W1, b1, W2, b2):
        import jax, jax.numpy as jnp
        import numpy as np
        B, T, D = (2, 1024, 768)
        H, HS = (12, 64)
        E, K = (8, 1)
        DF = 4 * D
        EPS = 1e-05

        def _ln(x, g, b):
            mu = jnp.mean(x, axis=-1, keepdims=True)
            var = jnp.mean(jnp.square(x - mu), axis=-1, keepdims=True)
            return (x - mu) * jax.lax.rsqrt(var + EPS) * g + b
        b, t, d = x.shape
        h = _ln(x, ln1_g, ln1_b)
        q = jnp.einsum('btd,hds->bhts', h, Wq)
        k = jnp.einsum('btd,hds->bhts', h, Wk)
        v = jnp.einsum('btd,hds->bhts', h, Wv)
        scores = jnp.einsum('bhts,bhus->bhtu', q, k) * d ** (-0.5)
        causal = jnp.tril(jnp.ones((t, t), dtype=bool))
        scores = jnp.where(causal, scores, -jnp.inf)
        att = jax.nn.softmax(scores, axis=-1)
        out = jnp.einsum('bhtu,bhus->bhts', att, v)
        out = out.transpose(0, 2, 1, 3).reshape(b, t, d)
        x = x + out @ Wp + bp
        h2 = _ln(x, ln2_g, ln2_b).reshape(-1, d)
        gate_logits = h2 @ Wg
        w, sel = jax.lax.top_k(gate_logits, K)
        w = jax.nn.softmax(w.astype(jnp.float32), axis=-1).astype(x.dtype)
        n = h2.shape[0]
        combine = jnp.zeros((n, Wg.shape[1]), x.dtype).at[jnp.arange(n)[:, None], sel].add(w)
        hid = jax.nn.relu(jnp.einsum('nd,edf->enf', h2, W1) + b1[:, None, :])
        y = jnp.einsum('enf,efd->end', hid, W2) + b2[:, None, :]
        moe = jnp.einsum('ne,end->nd', combine, y)
        return x + moe.reshape(b, t, d)
    edge_index = jnp.stack([src, dst])
    x = x + _L0_gnn_ref(_layernorm(x, axis=-1), edge_index, L0_gnn_W1, L0_gnn_a_src1, L0_gnn_a_dst1, L0_gnn_b1, L0_gnn_g1, L0_gnn_be1, L0_gnn_Wr1, L0_gnn_br1, L0_gnn_W2, L0_gnn_a_src2, L0_gnn_a_dst2, L0_gnn_b2, L0_gnn_g2, L0_gnn_be2, L0_gnn_Wr2, L0_gnn_br2)
    x = x + _L0_ffn_ref(_layernorm(x, axis=-1)[None], L0_ffn_ln1_g, L0_ffn_ln1_b, L0_ffn_ln2_g, L0_ffn_ln2_b, L0_ffn_Wq, L0_ffn_Wk, L0_ffn_Wv, L0_ffn_Wp, L0_ffn_bp, L0_ffn_Wg, L0_ffn_W1, L0_ffn_b1, L0_ffn_W2, L0_ffn_b2)[0]
    return x

_drawn_inputs = setup_inputs


def setup_inputs(seed=0):
    import zlib

    import numpy as np

    out = dict(_drawn_inputs(seed))
    spreads = {'L0_gnn_b1': (0.0, 0.1),
     'L0_gnn_g1': (1.0, 0.2),
     'L0_gnn_be1': (0.0, 0.1),
     'L0_gnn_br1': (0.0, 0.1),
     'L0_gnn_b2': (0.0, 0.1),
     'L0_gnn_g2': (1.0, 0.2),
     'L0_gnn_be2': (0.0, 0.1),
     'L0_gnn_br2': (0.0, 0.1),
     'L0_ffn_ln1_g': (1.0, 0.2),
     'L0_ffn_ln1_b': (0.0, 0.1),
     'L0_ffn_ln2_g': (1.0, 0.2),
     'L0_ffn_ln2_b': (0.0, 0.1),
     'L0_ffn_bp': (0.0, 0.1),
     'L0_ffn_b1': (0.0, 0.269),
     'L0_ffn_b2': (0.0, 0.1)}
    factors = {'L0_ffn_Wq': 8.0, 'L0_ffn_Wk': 8.0, 'L0_gnn_a_dst2': 3.244}
    for name, (base, spread) in spreads.items():
        noise = np.random.default_rng([zlib.crc32(name.encode()), seed]).standard_normal(out[name].shape)
        drawn = base * np.exp(spread * noise) if base else spread * noise
        out[name] = jnp.asarray(drawn.astype(out[name].dtype))
    for name, factor in factors.items():
        out[name] = (out[name] * factor).astype(out[name].dtype)
    return out
```

```python
from contextlib import ExitStack

import concourse.bass as bass
from concourse import mybir

F32, F16, I32, U32 = mybir.dt.float32, mybir.dt.float16, mybir.dt.int32, mybir.dt.uint32
ACT = mybir.ActivationFunctionType
ALU = mybir.AluOpType
AX_X = mybir.AxisListType.X
BIG = 1e30
BANK = 512
SLOT = 2 * BANK
SLOTS = 4


def item_plan(T, HEADS, FH, FC):
    plan = [(("edges",), "D"), (("bounds",), "D")]
    plan += [(("x0T", t), "AD"[t % 2]) for t in range(T)]
    plan += [(("xl1", t), "A") for t in range(T)]
    plan += [(("res1", t), "D") for t in range(T)]
    plan += [(("count", t), "D") for t in range(T)]
    for layer, heads in ((1, HEADS), (2, 1)):
        if layer == 2:
            plan += [(("h1T", t), "AD"[t % 2]) for t in range(T)]
            plan += [(("xl2", t), "A") for t in range(T)]
            plan += [(("res2", t), "D") for t in range(T)]
        n = heads * T
        for i in range(n + 2):
            if i < n and i % T == 0:
                plan.append((("src_row", layer, i // T), "A"))
            if 1 <= i <= n:
                plan.append((("probT", layer, i - 1), "A"))
            if i >= 2:
                plan.append((("agg", layer, i - 2), "D"))
    plan += [(("hT", t), "AD"[t % 2]) for t in range(T)]
    plan += [(("QT", c), "A") for c in range(FC)] + [(("KT", c), "D") for c in range(FC)]
    plan += [(("V", t), "A") for t in range(T)]
    n = T * FH
    for i in range(n + 2):
        if i < n:
            plan.append((("score", i), "D"))
        if 1 <= i <= n:
            plan.append((("attT", i - 1), "A"))
        if i >= 2:
            plan.append((("pv", i - 2), "D"))
    plan += [(("OT", t), "AD"[t % 2]) for t in range(T)]
    plan += [(("proj", t), "D") for t in range(T)]
    plan += [(("b1T",), "A")]
    plan += [(("h2T", t), "AD"[t % 2]) for t in range(T)]
    plan += [(("gate",), "D"), (("rank",), "D"), (("selT",), "D")]
    plan += [(("b2sum", t), "D") for t in range(T)]
    return plan


def gnn_moe_kernel(nc, x, src, dst, g_W1, g_as1, g_ad1, g_b1, g_g1, g_be1, g_Wr1, g_br1, g_W2, g_as2, g_ad2,
                   g_b2, g_g2, g_be2, g_Wr2, g_br2, ln1_g, ln1_b, ln2_g, ln2_b, Wq, Wk, Wv, Wp, bp, Wg,
                   W1, b1, W2, b2, out):
    N, D = x.shape
    NE = src.shape[0]
    P = 125
    T = N // P
    HEADS, HID = g_as1.shape
    HC = HEADS * HID
    FH, _, HS = Wq.shape
    E, _, DF = W1.shape
    KD, KH = D // 128, HC // 128
    FC = FH * HS // 128
    G, J = 40, NE // (40 * P)
    assert T * P == N and G * J * P == NE and FC * 128 == FH * HS and HS == 64
    SCALE = float(D) ** -0.5
    EPS = 1e-5
    C, CW = 6, DF // 6
    CK = CW // 128
    assert CW == BANK and C % 2 == 0
    BR = 128
    NB = T + E - 1
    assert BR * T >= N

    plan = item_plan(T, HEADS, FH, FC)
    item = {name: n for n, (name, _) in enumerate(plan)}
    emptied = []
    for n, (_, who) in enumerate(plan):
        emptied.append((who, sum(w == who for _, w in plan[:n + 1])))

    hs_dram = nc.dram_tensor("sorted_tokens", [(NB + 1) * BR, D], F32, kind="Internal").ap()
    ys_dram = nc.dram_tensor("sorted_results", [(NB + 1) * BR, D], F32, kind="Internal").ap()

    with ExitStack() as ctx:
        def sem(name):
            return ctx.enter_context(nc.semaphore(name))

        SW = 6144
        area = ctx.enter_context(nc.sbuf_tensor("area", [128, 6 * SW], F32))
        TW, XW, CWD = KH * N, T * D, T * N
        low = ctx.enter_context(nc.sbuf_tensor("low", [128, TW + 2 * XW + CWD], F32))
        psum = ctx.enter_context(nc.psum_tensor("psum", [128, SLOTS * SLOT], F32))

        def A(slot, at, n, parts=128):
            return area[0:parts, slot * SW + at:slot * SW + at + n]

        def v3(ap, a):
            return ap.rearrange("p (a b) -> p a b", a=a)

        T_ = low[:, 0:TW]
        X_ = low[0:P, TW:TW + XW]
        S_ = low[0:P, TW + XW:TW + 2 * XW]
        C_ = low[0:P, TW + 2 * XW:TW + 2 * XW + CWD]
        aT6, aT8 = v3(T_[:, 0:KD * N], KD), v3(T_, KH)
        tok = v3(X_, T)
        total = v3(S_, T)
        counts = v3(C_, T)
        absent = v3(low[0:P, TW + XW:TW + XW + CWD], T)
        zbuf = [low[0:P, TW + i * N:TW + (i + 1) * N] for i in range(4)]
        x_again = v3(low[0:P, 0:XW], T)

        w1_g, wr1_g = v3(A(0, 0, KD * HC), KD), v3(A(1, 0, KD * HC), KD)
        w2_g, wr2_g = v3(A(0, 0, KH * D), KH), v3(A(1, 0, KH * D), KH)
        row_a = [A(2, 0, HC, P), A(2, HC, HC, P)]
        oh_src = v3(A(2, 2048, J * 626 // 2, P).bitcast(F16), J)[:, :, 0:N]
        oh_dst = v3(A(2, 3300, J * 128 // 2, P).bitcast(F16), J)[:, :, 0:P]
        iota16 = A(2, 3556, 313, P).bitcast(F16)
        zero16 = A(2, 3869, BANK // 2).bitcast(F16)
        edge_i = v3(A(2, 4125, 2 * J * P, G).bitcast(I32), 2)
        edge_f = v3(A(2, 5125, 2 * J * P, G), 2)
        agg1 = v3(A(2, 0, T * HC, P), T)
        agg2 = v3(A(2, 0, T * D, P), T)
        row1 = {n: A(3, i * HC, HC, P) for i, n in enumerate(("br1", "b1", "g1", "be1"))}
        row2 = {n: A(3, i * D, D, P) for i, n in enumerate(("br2", "b2", "g2", "be2"))}
        probT = [v3(A(3, 4096 + i * N, N, P), T) for i in range(2)]
        eT = A(3, 4096 + 2 * N, 2 * J * 2 * G, P).rearrange("p (a j g) -> p a j g", a=2, j=J)
        xl1, xl2 = v3(A(4, 0, T * HC, P), T), v3(A(4, 0, T * D, P), T)
        src_row = [A(4, T * HC, N, P), A(5, T * HC, N, P)]
        res1, res2 = v3(A(5, 0, T * HC, P), T), v3(A(5, 0, T * D, P), T)
        row_a2 = [A(2, 4096, D, P), A(2, 4096 + D, D, P)]
        wq_s, wk_s, wv_s, wp_s = (v3(A(s, 0, KD * D), KD) for s in (0, 1, 4, 1))
        QT, KT = v3(A(5, 0, FC * N), FC), v3(A(3, 0, FC * N), FC)
        Vt, O = v3(A(2, 0, T * D, P), T), v3(A(0, 0, T * D, P), T)
        causal = A(3, FC * N, N, P)
        bp_row = A(3, FC * N + N, D, P)
        abuf = [low[0:P, TW + 2 * XW + i * N:TW + 2 * XW + (i + 1) * N] for i in range(3)]
        attT = [v3(low[0:P, TW + 2 * XW + (3 + i) * N:TW + 2 * XW + (4 + i) * N], T) for i in range(2)]
        n2 = v3(A(5, 0, T * D, P), T)
        h2T = v3(A(4, 0, KD * N), KD)
        b2_s = A(2, 4096, D, E)
        b1_rows = A(2, 4096 + D, 2 * 128, 96)
        w1_s = [v3(A(c, 0, KD * CW), KD) for c in range(C)]
        w2_s = [v3(A(c, KD * CW, CK * D), CK) for c in range(C)]
        xt = T_[:, 0:D]
        ht = v3(T_[:, D:D + KD * BR], KD)
        hid = [T_[:, 2 * D + i * CW:2 * D + (i + 1) * CW] for i in range(2)]
        hidT = [v3(T_[:, 2 * D + (2 + i) * CW:2 * D + (3 + i) * CW], CK) for i in range(2)]
        y_o = T_[:, 2 * D + 4 * CW:3 * D + 4 * CW]
        back = v3(C_[:, 0:3 * D], 3)
        back = [back[:, i, :] for i in range(3)] + [X_[:, 0:D], X_[:, D:2 * D]]

        smalls = ctx.enter_context(nc.sbuf_tensor("smalls", [128, 512], F32))
        carved = [0]

        def small(parts, *shape, dt=F32):
            n = 1
            for k in shape:
                n *= k
            v = smalls[0:parts, carved[0]:carved[0] + n]
            carved[0] += n
            assert carved[0] <= 512
            if dt is not F32:
                v = v.bitcast(dt)
            return v3(v, shape[0]) if len(shape) == 2 else v

        ident, ones = small(128, 128), small(128, 128)
        stats, mv = small(P, T, 12), small(P, T, 2)
        rstd, half = small(P, T), small(P, T)
        a_src, a_dst = small(P, T, HEADS), small(P, T, HEADS)
        negm, rsum, rinv = small(P, 4), small(P, 4), small(P, 4)
        cols = small(128, 4, KD)
        wg_s = small(128, KD, E)
        pos_i = small(P, T, dt=U32)
        tab = small(1, 3, E, dt=I32)
        nact, nblocks = small(1, 1, dt=I32), small(1, 1, dt=I32)
        at3 = 4096 + 2 * N + 4 * J * G
        g_i, mm_s, v_b = A(3, at3, 2, G), A(3, at3 + 2, 2, G), A(3, at3 + 4, 2 * T, G)
        h_a, h_b = A(3, at3 + 14, 1, G), A(3, at3 + 15, 1, G)
        vm, rr, ri = A(3, at3 + 16, 1, 2 * T), A(3, at3 + 17, 2 * T, 1), A(3, at3 + 27, 2 * T, 1).bitcast(I32)
        assert at3 + 40 <= SW
        at2 = [5120]

        def scratch(parts, *shape):
            n = shape[0] * (shape[1] if len(shape) == 2 else 1)
            v = A(2, at2[0], n, parts)
            at2[0] += n
            assert at2[0] <= SW
            return v3(v, shape[0]) if len(shape) == 2 else v

        lg, sel, cum = scratch(P, T, E), scratch(P, T, E), scratch(P, T + 1, E)
        tmx, pos_f = scratch(P, T), scratch(P, T)
        iota8, desc8, zero8 = scratch(P, E), scratch(P, E), scratch(P, E)
        nblk, nblk_sum, start, active, active_sum, order, base8, junk8 = (scratch(P, E) for _ in range(8))
        match, prod, tab_f = scratch(1, E, E), scratch(1, E, E), scratch(1, 3, E)
        before = A(3, FC * N + N + D, P, P)
        selT = A(2, 0, N, E)
        b1T = T_[:, 4400:4400 + E * DF // 128]

        x_in, edges_in, rows1_in, rows2_in = sem("x_in"), sem("edges_in"), sem("rows1_in"), sem("rows2_in")
        arows1_in, arows2_in, x2_in, small_in = sem("arows1_in"), sem("arows2_in"), sem("x2_in"), sem("small_in")
        w1g_in, wr1g_in, w2g_in, wr2g_in = sem("w1g_in"), sem("wr1g_in"), sem("w2g_in"), sem("wr2g_in")
        wq_in, wk_in, wv_in, wp_in, late_in = sem("wq_in"), sem("wk_in"), sem("wv_in"), sem("wp_in"), sem("late_in")
        consts = sem("consts")
        made = sem("made")
        act_emptied, dve_emptied = sem("act_emptied"), sem("dve_emptied")
        step = sem("step")
        pstep = sem("pstep")
        bounds_v, bounds_r, edge_ready = sem("bounds_v"), sem("bounds_r"), sem("edge_ready")
        oh_ready = [sem(f"oh_ready{d}") for d in range(T)]
        oh_used = [sem(f"oh_used{d}") for d in range(T)]
        var_ok, rstd_ok = sem("var_ok"), sem("rstd_ok")
        ln_done = {n: sem(f"ln_{n}") for n in ("x0", "n1", "n2")}
        row_ok, pair_ok, neg_ok, exp_ok, prob_ok = (sem(n) for n in ("row_ok", "pair_ok", "neg_ok", "exp_ok", "prob_ok"))
        epi_a, epi_b, epi_c = sem("epi_a"), sem("epi_b"), sem("epi_c")
        sc_exp = sem("sc_exp")
        y1_ok, routed, padded, scattered = sem("y1_ok"), sem("routed"), sem("padded"), sem("scattered")
        w1_in = [sem(f"w1_in{c}") for c in range(C)]
        w2_in = [sem(f"w2_in{c}") for c in range(C)]
        xt_in, xt_used, xtT, ht_ok = sem("xt_in"), sem("xt_used"), sem("xtT"), sem("ht_ok")
        hid_mm, hid_cp, hid_tr, hid_relu, hid_used = (sem(n) for n in ("hid_mm", "hid_cp", "hid_tr", "hid_relu", "hid_used"))
        y_cp, y_out = sem("y_cp"), sem("y_out")
        gathered = [sem(f"gathered{t}") for t in range(T)]
        final, stored, sel_ok = sem("final"), sem("stored"), sem("sel_ok")
        y_stored, all_stored = sem("y_stored"), sem("all_stored")

        def place(name, n=SLOT, parts=128):
            s = item[name] % SLOTS
            return psum[0:parts, s * SLOT:s * SLOT + n]

        def free(pe, name):
            if item[name] >= SLOTS:
                who, n = emptied[item[name] - SLOTS]
                pe.wait_ge(act_emptied if who == "A" else dve_emptied, n)

        def done(eng, name):
            eng.wait_ge(made, item[name] + 1)

        def was_emptied(eng, name):
            who, n = emptied[item[name]]
            eng.wait_ge(act_emptied if who == "A" else dve_emptied, n)

        def tview(name, k, n, parts=128):
            return v3(place(name, k * 128, parts), k)[:, :, 0:n]

        def bcast(row, parts):
            return bass.AP(tensor=row.tensor, offset=row.offset, ap=[[0, parts], [1, row.shape[0]]])

        def spread(ap, shape, keep):
            steps = [[0, shape[1]], [0, shape[2]]]
            steps[keep - 1] = [1, shape[keep]]
            return bass.AP(tensor=ap.tensor, offset=ap.offset, ap=[[ap.ap[0][0], shape[0]], *steps])

        block = ctx.enter_context(nc.Block())

        @block.sync
        def _(sp):
            sp.dma_start(edge_i[:, 0, :], src.rearrange("(g n) -> g n", g=G)).then_inc(edges_in, 16)
            sp.dma_start(edge_i[:, 1, :], dst.rearrange("(g n) -> g n", g=G)).then_inc(edges_in, 16)
            for t in range(T):
                sp.dma_start(tok[:, t, :], x[t * P:(t + 1) * P, :]).then_inc(x_in, 16)
            sp.dma_start(w1_g, g_W1.rearrange("(k p) n -> p k n", p=128)).then_inc(w1g_in, 16)
            sp.dma_start(wr1_g, g_Wr1.rearrange("(k p) n -> p k n", p=128)).then_inc(wr1g_in, 16)
            for r, a in zip(row_a, (g_as1, g_ad1)):
                sp.dma_start(r, bcast(a.rearrange("h c -> (h c)"), P)).then_inc(arows1_in, 16)
            for n, a in (("br1", g_br1), ("b1", g_b1), ("g1", g_g1), ("be1", g_be1)):
                sp.dma_start(row1[n], bcast(a, P)).then_inc(rows1_in, 16)
            for i, a in enumerate((ln1_g, ln1_b, ln2_g, ln2_b)):
                sp.dma_start(cols[:, i, :], a.rearrange("(k p) -> p k", p=128),
                             allow_slow_non_contiguous=True).then_inc(small_in, 16)
            sp.dma_start(wg_s[:, :, :], Wg.rearrange("(k p) e -> p k e", p=128)).then_inc(small_in, 16)
            done(sp, ("xl1", T - 1))
            sp.dma_start(w2_g, g_W2.rearrange("(k p) n -> p k n", p=128)).then_inc(w2g_in, 16)
            done(sp, ("res1", T - 1))
            sp.dma_start(wr2_g, g_Wr2.rearrange("(k p) n -> p k n", p=128)).then_inc(wr2g_in, 16)
            sp.wait_ge(epi_c, T)
            for n, a in (("br2", g_br2), ("b2", g_b2), ("g2", g_g2), ("be2", g_be2)):
                sp.dma_start(row2[n], bcast(a, P)).then_inc(rows2_in, 16)
            for r, a in zip(row_a2, (g_as2, g_ad2)):
                sp.dma_start(r, bcast(a.rearrange("h c -> (h c)"), P)).then_inc(arows2_in, 16)
            done(sp, ("xl2", T - 1))
            for k in range(KD):
                sp.dma_start(wq_s[:, k, :].rearrange("p (h s) -> p h s", h=FH),
                             Wq[:, k * 128:(k + 1) * 128, :].rearrange("h p s -> p h s")).then_inc(wq_in, 16)
            done(sp, ("res2", T - 1))
            sp.dma_start(x_again, x.rearrange("(t p) d -> p t d", p=P)).then_inc(x2_in, 16)
            for k in range(KD):
                sp.dma_start(wk_s[:, k, :].rearrange("p (h s) -> p h s", h=FH),
                             Wk[:, k * 128:(k + 1) * 128, :].rearrange("h p s -> p h s")).then_inc(wk_in, 16)
            done(sp, ("agg", 2, T - 1))
            for k in range(KD):
                sp.dma_start(wv_s[:, k, :].rearrange("p (h s) -> p h s", h=FH),
                             Wv[:, k * 128:(k + 1) * 128, :].rearrange("h p s -> p h s")).then_inc(wv_in, 16)
            done(sp, ("KT", FC - 1))
            sp.dma_start(wp_s, Wp.rearrange("(k p) n -> p k n", p=128)).then_inc(wp_in, 16)
            sp.dma_start(bp_row, bcast(bp, P)).then_inc(late_in, 16)
            sp.dma_start(b2_s, b2).then_inc(late_in, 16)
            sp.dma_start(v3(b1_rows, 2), b1.rearrange("e f -> (e f)").rearrange("(a r c) -> r a c", a=2, c=128)).then_inc(late_in, 16)
            sp.wait_ge(routed, 1)
            n_active = sp.value_load(nact[0:1, 0:1], min_val=1, max_val=E)
            last_use = {0: ("OT", T - 1), 1: ("proj", T - 1), 2: ("b2sum", T - 1), 3: ("rank",), 4: ("gate",),
                        5: ("b2sum", T - 1)}
            with sp.Fori(0, n_active) as a:
                e = sp.value_load(tab[0:1, 0, bass.ds(a, 1)], min_val=0, max_val=E - 1)
                first = sp.value_load(tab[0:1, 2, bass.ds(a, 1)], min_val=0, max_val=NB - 1)
                for c in range(C):
                    done(sp, last_use[c])
                    if c == 5:
                        sp.wait_ge(scattered, 16 * T)
                    sp.wait_ge(hid_mm, first * C + (c + 1))
                    sp.dma_start(w1_s[c], W1[bass.ds(e, 1), :, c * CW:(c + 1) * CW]
                                 .rearrange("a (k p) n -> p (a k) n", p=128)).then_inc(w1_in[c], 16)
                    sp.wait_ge(hid_used, first * C + (c + 1))
                    sp.dma_start(w2_s[c], W2[bass.ds(e, 1), c * CW:(c + 1) * CW, :]
                                 .rearrange("a (k p) n -> p (a k) n", p=128)).then_inc(w2_in[c], 16)
            for t in range(T):
                sp.wait_ge(final, t + 2)
                sp.dma_start(out[t * P:(t + 1) * P, :], total[:, t, :]).then_inc(stored, 16)
            sp.wait_ge(stored, 16 * T)

        @block.gpsimd
        def _(pool):
            n = [0]

            def link(ins):
                n[0] += 1
                ins.then_inc(pstep, 1)
                pool.wait_ge(pstep, n[0])

            link(pool.memset(ones, 0.0))
            link(pool.affine_select(out=ident, in_=ones, compare_op=ALU.not_equal, fill=1.0, base=0,
                                    pattern=[[-1, 128]], channel_multiplier=1))
            link(pool.memset(ones, 1.0))
            link(pool.memset(zero16, 0.0))
            link(pool.memset(half, -0.5))
            link(pool.iota(iota16[:, 0:N], pattern=[[1, N]], base=0, channel_multiplier=0,
                           allow_small_or_imprecise_dtypes=True))
            link(pool.iota(g_i[:, 0:1], pattern=[[1, 1]], base=1, channel_multiplier=1,
                           allow_small_or_imprecise_dtypes=True))
            pool.iota(g_i[:, 1:2], pattern=[[1, 1]], base=G, channel_multiplier=-1,
                      allow_small_or_imprecise_dtypes=True).then_inc(consts, 1)
            zeros = zero16.bitcast(F32)
            zsrc = bass.AP(tensor=zeros.tensor, offset=zeros.offset, ap=[[zeros.ap[0][0], 128], [0, NB + 1], [1, 256]])
            for rows in (hs_dram, ys_dram):
                for c in range(0, D, 256):
                    pool.dma_start(rows.rearrange("(q p) n -> p q n", p=BR)[:, :, c:c + 256],
                                   zsrc).then_inc(padded, 16)

            def inverse_root(k):
                pool.wait_ge(var_ok, k + 1)
                link(pool.tensor_scalar(rstd, mv[:, :, 1], EPS, None, ALU.add))
                pool.tensor_tensor(rstd, rstd, half, ALU.pow).then_inc(rstd_ok, 1)

            inverse_root(0)
            inverse_root(1)
            pool.wait_ge(rows1_in, 64)
            for t in range(T):
                pool.wait_ge(epi_a, t + 1)
                link(pool.tensor_tensor(agg1[:, t, :], agg1[:, t, :], row1["g1"], ALU.mult))
                pool.tensor_tensor(agg1[:, t, :], agg1[:, t, :], row1["be1"], ALU.add).then_inc(epi_b, 1)
            inverse_root(2)
            pool.wait_ge(rows2_in, 64)
            for t in range(T):
                pool.wait_ge(epi_a, T + t + 1)
                link(pool.tensor_tensor(agg2[:, t, :], agg2[:, t, :], row2["g2"], ALU.mult))
                link(pool.tensor_tensor(agg2[:, t, :], agg2[:, t, :], row2["be2"], ALU.add))
                pool.tensor_tensor(agg2[:, t, :], agg2[:, t, :], res2[:, t, :], ALU.add).then_inc(epi_b, 1)
            inverse_root(3)
            inverse_root(4)
            was_emptied(pool, ("hT", T - 1))
            was_emptied(pool, ("hT", T - 2))
            link(pool.memset(causal, 0.0))
            link(pool.affine_select(out=causal[:, N - P:N], in_=causal[:, N - P:N], compare_op=ALU.is_ge, fill=-BIG,
                                    base=0, pattern=[[-1, P]], channel_multiplier=1))
            link(pool.memset(before, 1.0))
            link(pool.affine_select(out=before, in_=before, compare_op=ALU.is_gt, fill=0.0,
                                    base=0, pattern=[[1, P]], channel_multiplier=-1))
            link(pool.memset(zero8, 0.0))
            link(pool.iota(iota8, pattern=[[1, E]], base=0, channel_multiplier=0, allow_small_or_imprecise_dtypes=True))
            pool.iota(desc8, pattern=[[-1, E]], base=E, channel_multiplier=0,
                      allow_small_or_imprecise_dtypes=True).then_inc(consts, 1)
            inverse_root(5)
            pool.wait_ge(padded, 32 * (D // 256))
            pool.wait_ge(ln_done["n2"], T)
            pool.wait_ge(routed, 1)
            for t in range(T):
                pool.indirect_dma_start(hs_dram, bass.IndirectOffsetOnAxis(ap=pos_i[:, t:t + 1], axis=0),
                                        n2[:, t, :], None).then_inc(scattered, 16)
            pool.wait_ge(scattered, 16 * T)
            was_emptied(pool, ("b1T",))
            pool.sem_inc(y_stored, 1)
            pool.dma_start(xt, hs_dram[0:BR, :]).then_inc(xt_in, 16)
            blocks = pool.value_load(nblocks[0:1, 0:1], min_val=1, max_val=NB)
            with pool.Fori(0, blocks) as b:
                pool.wait_ge(xt_used, b + 1)
                pool.dma_start(xt, hs_dram[bass.ds(b * BR + BR, BR), :]).then_inc(xt_in, 16)
                pool.wait_ge(y_cp, b + 2)
                pool.dma_start(ys_dram[bass.ds(b * BR, BR), :], y_o).then_inc(y_out, 16)
                pool.wait_ge(y_out, b * 16 + 16)
                pool.sem_inc(y_stored, 1)
            pool.wait_ge(xt_in, blocks * 16 + 16)
            pool.sem_inc(all_stored, 1)
            pool.wait_ge(all_stored, 1)
            pool.wait_ge(final, 1)
            for t in range(T):
                pool.indirect_dma_start(back[t], None, ys_dram,
                                        bass.IndirectOffsetOnAxis(ap=pos_i[:, t:t + 1], axis=0)).then_inc(gathered[t], 16)

        @block.scalar
        def _(act):
            last = [-1]

            def emptied_by(name, ins):
                assert plan[item[name]][1] == "A" and item[name] > last[0]
                last[0] = item[name]
                ins.then_inc(act_emptied, 1)

            def copy(name, dst, src):
                done(act, name)
                emptied_by(name, act.activation(dst, src, ACT.Copy))

            for t in range(T):
                if plan[item["x0T", t]][1] == "A":
                    copy(("x0T", t), aT6[:, :, t * P:(t + 1) * P], tview(("x0T", t), KD, P))
            for t in range(T):
                copy(("xl1", t), xl1[:, t, :], place(("xl1", t), HC, P))
            for layer, heads in ((1, HEADS), (2, 1)):
                if layer == 2:
                    for t in range(T):
                        if plan[item["h1T", t]][1] == "A":
                            copy(("h1T", t), aT8[:, :, t * P:(t + 1) * P], tview(("h1T", t), KH, P))
                    for t in range(T):
                        copy(("xl2", t), xl2[:, t, :], place(("xl2", t), D, P))
                n, before_ = heads * T, 0 if layer == 1 else HEADS * T
                for i in range(n + 2):
                    g = before_ + i
                    if i >= 2:
                        if i >= 4:
                            done(act, ("agg", layer, i - 4))
                        copy(("probT", layer, i - 2), probT[i % 2], tview(("probT", layer, i - 2), T, P, P))
                    if i < n:
                        h, t = divmod(i, T)
                        if t == 0:
                            copy(("src_row", layer, h), src_row[h % 2], place(("src_row", layer, h), N, P))
                            act.wait_ge(act_emptied, emptied[item["src_row", layer, h]][1])
                        if i >= 4:
                            done(act, ("probT", layer, i - 4))
                        act.activation(zbuf[g % 4], src_row[h % 2], ACT.Identity,
                                       bias=a_dst[:, t, h:h + 1]).then_inc(pair_ok, 1)
                    if 1 <= i <= n:
                        act.wait_ge(neg_ok, g)
                        act.activation(zbuf[(g - 1) % 4], zbuf[(g - 1) % 4], ACT.Exp, scale=-1.0,
                                       bias=negm[:, (g - 1) % 4:(g - 1) % 4 + 1]).then_inc(exp_ok, 1)
            for t in range(T):
                if plan[item["hT", t]][1] == "A":
                    done(act, ("hT", t))
                    for k in range(KD):
                        ins = act.activation(aT6[:, k, t * P:(t + 1) * P], tview(("hT", t), KD, P)[:, k, :],
                                             ACT.Identity, scale=cols[:, 0, k:k + 1], bias=cols[:, 1, k:k + 1])
                    emptied_by(("hT", t), ins)
            for c in range(FC):
                copy(("QT", c), QT[:, c, :], place(("QT", c), N))
            for t in range(T):
                copy(("V", t), Vt[:, t, :], place(("V", t), D, P))
            n = T * FH
            for i in range(n + 2):
                if i < n:
                    was_emptied(act, ("score", i))
                    if i >= 4:
                        act.wait_ge(dve_emptied, emptied[item["pv", i - 4]][1])
                    w = (i // FH + 1) * P
                    act.activation(abuf[i % 3][:, 0:w], abuf[i % 3][:, 0:w], ACT.Exp, scale=-1.0,
                                   bias=negm[:, i % 4:i % 4 + 1],
                                   accum_out=rsum[:, i % 4:i % 4 + 1]).then_inc(sc_exp, 1)
                if 1 <= i <= n:
                    if i >= 3:
                        done(act, ("pv", i - 3))
                    k = (i - 1) // FH + 1
                    copy(("attT", i - 1), attT[(i - 1) % 2][:, 0:k, :], tview(("attT", i - 1), k, P, P))
            for t in range(T):
                if plan[item["OT", t]][1] == "A":
                    copy(("OT", t), aT6[:, :, t * P:(t + 1) * P], tview(("OT", t), KD, P))
            done(act, ("proj", T - 1))
            copy(("b1T",), v3(b1T, 2), v3(place(("b1T",), 256), 2)[:, :, 0:96])
            for t in range(T):
                if plan[item["h2T", t]][1] == "A":
                    done(act, ("h2T", t))
                    for k in range(KD):
                        ins = act.activation(h2T[:, k, t * P:(t + 1) * P], tview(("h2T", t), KD, P)[:, k, :],
                                             ACT.Identity, scale=cols[:, 2, k:k + 1], bias=cols[:, 3, k:k + 1])
                    emptied_by(("h2T", t), ins)
            act.wait_ge(routed, 1)
            n_active = act.value_load(nact[0:1, 0:1], min_val=1, max_val=E)
            act.sem_inc(hid_cp, 2)
            act.sem_inc(y_cp, 1)
            with act.Fori(0, n_active) as a:
                nb = act.value_load(tab[0:1, 1, bass.ds(a, 1)], min_val=1, max_val=T)
                first = act.value_load(tab[0:1, 2, bass.ds(a, 1)], min_val=0, max_val=NB - 1)
                with act.Fori(0, nb) as i:
                    b = first + i
                    for c in range(C):
                        act.wait_ge(hid_mm, b * C + (C + c + 1))
                        act.wait_ge(hid_tr, b * C + (c + 1))
                        act.activation(hid[c % 2], psum[:, (c % 2) * BANK:(c % 2 + 1) * BANK],
                                       ACT.Copy).then_inc(hid_cp, 1)
                    act.wait_ge(hid_used, b * C + 2 * C)
                    act.wait_ge(y_stored, b + 1)
                    act.activation(v3(y_o, 2), v3(psum[:, 4 * BANK:6 * BANK], 2)[:, :, 0:D // 2],
                                   ACT.Copy).then_inc(y_cp, 1)

        @block.vector
        def _(dve):
            n = [0]

            def link(ins):
                n[0] += 1
                ins.then_inc(step, 1)
                dve.wait_ge(step, n[0])

            last = [-1]

            def emptied_by(name, ins):
                assert plan[item[name]][1] == "D" and item[name] > last[0]
                last[0] = item[name]
                ins.then_inc(dve_emptied, 1)

            def variance(k, view, width):
                if k:
                    dve.wait_ge(rstd_ok, k)
                for t in range(T):
                    for q in range(2):
                        ins = dve.bn_stats(stats[:, t, 6 * q:6 * q + 6], view[:, t, q * width // 2:(q + 1) * width // 2])
                link(ins)
                for t in range(T):
                    ins = dve.bn_aggr(mv[:, t, :], stats[:, t, :])
                ins.then_inc(var_ok, 1)
                dve.wait_ge(rstd_ok, k + 1)

            def normal(out_, in_, t):
                return dve.tensor_scalar(out_, in_, mv[:, t, 0:1], rstd[:, t:t + 1], ALU.subtract, ALU.mult)

            dve.wait_ge(edges_in, 32)
            link(dve.tensor_copy(edge_f, edge_i))
            link(dve.tensor_reduce(mm_s[:, 0:1], edge_f[:, 1, :], AX_X, ALU.max))
            link(dve.tensor_reduce(mm_s[:, 1:2], edge_f[:, 1, :], AX_X, ALU.min))
            dve.wait_ge(consts, 1)
            for d in range(T):
                link(dve.tensor_scalar(h_a, mm_s[:, 0:1], float(P * d), None, ALU.is_ge))
                link(dve.tensor_scalar(h_b, mm_s[:, 1:2], float(P * d + P), None, ALU.is_lt))
                link(dve.tensor_tensor(h_a, h_a, h_b, ALU.mult))
                link(dve.tensor_scalar(v_b[:, 2 * d:2 * d + 2], g_i, h_a, None, ALU.mult))
            dve.sem_inc(bounds_v, 1)
            done(dve, ("edges",))
            dve.tensor_reduce(vm, place(("edges",))[0:2 * T, BANK:BANK + G], AX_X, ALU.max).then_inc(bounds_v, 1)
            emptied_by(("edges",), dve.tensor_copy(
                eT[:, :, :, 0:G], place(("edges",), 2 * J * G, P).rearrange("p (a j g) -> p a j g", a=2, j=J)))
            done(dve, ("bounds",))
            emptied_by(("bounds",), dve.tensor_copy(rr, place(("bounds",), 2 * T, 1)))
            was_emptied(dve, ("bounds",))
            rv = rr.rearrange("p (d a) -> p a d", a=2)
            link(dve.tensor_scalar(rv[:, 1, :], rv[:, 1, :], -1.0, float(G), ALU.mult, ALU.add))
            link(dve.tensor_scalar(rv[:, 1, :], rv[:, 1, :], float(G - 1), None, ALU.min))
            link(dve.tensor_tensor(rv[:, 0, :], rv[:, 0, :], rv[:, 1, :], ALU.subtract))
            link(dve.tensor_scalar(rv[:, 0, :], rv[:, 0, :], 1.0, None, ALU.max))
            dve.tensor_copy(ri, rr).then_inc(bounds_r, 1)

            dve.wait_ge(x_in, 16 * T)
            variance(0, tok, D)
            for t in range(T):
                normal(tok[:, t, :], tok[:, t, :], t).then_inc(ln_done["x0"], 1)
            for t in range(T):
                if plan[item["x0T", t]][1] == "D":
                    done(dve, ("x0T", t))
                    emptied_by(("x0T", t), dve.tensor_copy(aT6[:, :, t * P:(t + 1) * P], tview(("x0T", t), KD, P)))
            dve.wait_ge(arows1_in, 32)

            def attention_values(layer, t, heads, width, xl, rows):
                was_emptied(dve, (f"xl{layer}", t))
                for h in range(heads):
                    for q, (row, a) in enumerate(zip(rows, (a_src, a_dst))):
                        junk = TW + (2 * h + q) * width
                        ins = dve.tensor_tensor_reduce(low[0:P, junk:junk + width], xl[:, t, h * width:(h + 1) * width],
                                                       row[:, h * width:(h + 1) * width], 1.0, 0.0, ALU.mult,
                                                       ALU.add, a[:, t, h:h + 1])
                link(ins)

            for t in range(T):
                attention_values(1, t, HEADS, HID, xl1, row_a)
            dve.wait_ge(rows1_in, 64)
            for t in range(T):
                done(dve, ("res1", t))
                emptied_by(("res1", t), dve.tensor_tensor(res1[:, t, :], place(("res1", t), HC, P), row1["br1"], ALU.add))

            for d in range(T):
                lo = dve.value_load(ri[0:1, 2 * d + 1:2 * d + 2], min_val=0, max_val=G - 1)
                groups = dve.value_load(ri[0:1, 2 * d:2 * d + 1], min_val=1, max_val=G)
                with dve.Fori(0, groups) as i:
                    for j in range(J):
                        dve.wait_ge(oh_used[d], i * J + j + 1)
                        dve.tensor_scalar(oh_dst[:, j, :], iota16[:, P * d:P * d + P],
                                          eT[:, 1, j, bass.ds(lo + i, 1)], None, ALU.is_equal)
                        dve.tensor_scalar(oh_src[:, j, :], iota16[:, 0:N], eT[:, 0, j, bass.ds(lo + i, 1)], None,
                                          ALU.is_equal).then_inc(oh_ready[d], 1)
                done(dve, ("count", d))
                emptied_by(("count", d), dve.tensor_copy(counts[:, d, :], place(("count", d), N, P)))
                was_emptied(dve, ("count", d))
                diag = counts[:, d, P * d:P * d + P]
                link(dve.tensor_tensor(diag, diag, ident[0:P, 0:P], ALU.add))
                link(dve.tensor_scalar(absent[:, d, :], counts[:, d, :], 0.0, -BIG, ALU.is_equal, ALU.mult))

            diag_src = low[0:P, TW + XW + CWD:TW + XW + CWD + N]

            def source_diagonals(layer, h):
                if (layer, h) != (1, 0):
                    done(dve, ("src_row", *((layer, h - 1) if h else (1, HEADS - 1))))
                for t in range(T):
                    ins = dve.tensor_scalar(diag_src[:, t * P:(t + 1) * P], ident[0:P, 0:P], a_src[:, t, h:h + 1],
                                            None, ALU.mult)
                ins.then_inc(row_ok, 1)

            def graph_attention(layer, heads, width, agg, bias_row):
                n_, before_ = heads * T, 0 if layer == 1 else HEADS * T
                source_diagonals(layer, 0)
                for i in range(n_ + 3):
                    g = before_ + i
                    if i < n_:
                        dve.wait_ge(pair_ok, g + 1)
                        z = zbuf[g % 4]
                        link(dve.scalar_tensor_tensor(out=z, in0=z, scalar=0.2, in1=z, op0=ALU.mult, op1=ALU.max))
                        dve.tensor_tensor_reduce(z, z, absent[:, i % T, :], -1.0, 3e38, ALU.add, ALU.min,
                                                 negm[:, g % 4:g % 4 + 1]).then_inc(neg_ok, 1)
                        if i % T == 2 and i // T + 1 < heads:
                            source_diagonals(layer, i // T + 1)
                    if 1 <= i <= n_:
                        dve.wait_ge(exp_ok, g)
                        z, t = zbuf[(g - 1) % 4], (i - 1) % T
                        q = slice((g - 1) % 4, (g - 1) % 4 + 1)
                        dve.tensor_tensor_reduce(z, z, counts[:, t, :], 1.0, 0.0, ALU.mult, ALU.add,
                                                 rsum[:, q]).then_inc(prob_ok, 1)
                        dve.wait_ge(prob_ok, g)
                        link(dve.tensor_scalar(rsum[:, q], rsum[:, q], 1e-16, None, ALU.add))
                        link(dve.reciprocal(rinv[:, q], rsum[:, q]))
                    if i >= 3:
                        h, t = divmod(i - 3, T)
                        q = slice((g - 3) % 4, (g - 3) % 4 + 1)
                        done(dve, ("agg", layer, i - 3))
                        emptied_by(("agg", layer, i - 3), dve.scalar_tensor_tensor(
                            out=agg[:, t, h * width:(h + 1) * width], in0=place(("agg", layer, i - 3), width, P),
                            scalar=rinv[:, q], in1=bias_row[:, h * width:(h + 1) * width], op0=ALU.mult, op1=ALU.add))
                was_emptied(dve, ("agg", layer, n_ - 1))

            dve.wait_ge(padded, 32 * (D // 256))
            graph_attention(1, HEADS, HID, agg1, row1["b1"])
            variance(1, agg1, HC)
            for t in range(T):
                normal(agg1[:, t, :], agg1[:, t, :], t).then_inc(epi_a, 1)
            for t in range(T):
                dve.wait_ge(epi_b, t + 1)
                dve.scalar_tensor_tensor(out=res1[:, t, :], in0=agg1[:, t, :], scalar=0.0, in1=res1[:, t, :],
                                         op0=ALU.max, op1=ALU.add).then_inc(epi_c, 1)
            for t in range(T):
                if plan[item["h1T", t]][1] == "D":
                    done(dve, ("h1T", t))
                    emptied_by(("h1T", t), dve.tensor_copy(aT8[:, :, t * P:(t + 1) * P], tview(("h1T", t), KH, P)))
            dve.wait_ge(arows2_in, 32)
            for t in range(T):
                attention_values(2, t, 1, D, xl2, row_a2)
            dve.wait_ge(rows2_in, 64)
            for t in range(T):
                done(dve, ("res2", t))
                emptied_by(("res2", t), dve.tensor_tensor(res2[:, t, :], place(("res2", t), D, P), row2["br2"], ALU.add))
            graph_attention(2, 1, D, agg2, row2["b2"])
            variance(2, agg2, D)
            for t in range(T):
                normal(agg2[:, t, :], agg2[:, t, :], t).then_inc(epi_a, 1)
            dve.wait_ge(x2_in, 16)
            for t in range(T):
                dve.wait_ge(epi_b, T + t + 1)
                ins = dve.tensor_tensor(total[:, t, :], agg2[:, t, :], x_again[:, t, :], ALU.add)
            link(ins)
            variance(3, total, D)
            for t in range(T):
                ins = normal(tok[:, t, :], total[:, t, :], t)
            link(ins)
            variance(4, tok, D)
            for t in range(T):
                normal(agg2[:, t, :], tok[:, t, :], t).then_inc(ln_done["n1"], 1)
            dve.wait_ge(small_in, 80)

            def affine_T(name, t, dst, g):
                if plan[item[name, t]][1] == "D":
                    done(dve, (name, t))
                    for k in range(KD):
                        ins = dve.tensor_scalar(dst[:, k, t * P:(t + 1) * P], tview((name, t), KD, P)[:, k, :],
                                                cols[:, g, k:k + 1], cols[:, g + 1, k:k + 1], ALU.mult, ALU.add)
                    emptied_by((name, t), ins)

            for t in range(T):
                affine_T("hT", t, aT6, 0)
            for c in range(FC):
                done(dve, ("KT", c))
                emptied_by(("KT", c), dve.tensor_copy(KT[:, c, :], place(("KT", c), N)))
            dve.wait_ge(consts, 2)
            n_ = T * FH
            for i in range(n_ + 2):
                if i < n_:
                    w = (i // FH + 1) * P
                    done(dve, ("score", i))
                    if i >= 3:
                        done(dve, ("attT", i - 3))
                    emptied_by(("score", i), dve.tensor_tensor_reduce(
                        abuf[i % 3][:, 0:w], place(("score", i), w, P), causal[:, N - w:N], -SCALE, 3e38,
                        ALU.add, ALU.min, negm[:, i % 4:i % 4 + 1]))
                if i >= 2:
                    t, h = divmod(i - 2, FH)
                    q = slice((i - 2) % 4, (i - 2) % 4 + 1)
                    dve.wait_ge(sc_exp, i - 1)
                    link(dve.reciprocal(rinv[:, q], rsum[:, q]))
                    done(dve, ("pv", i - 2))
                    emptied_by(("pv", i - 2), dve.tensor_scalar(O[:, t, h * HS:(h + 1) * HS],
                                                                place(("pv", i - 2), HS, P), rinv[:, q], None, ALU.mult))
            for t in range(T):
                if plan[item["OT", t]][1] == "D":
                    done(dve, ("OT", t))
                    emptied_by(("OT", t), dve.tensor_copy(aT6[:, :, t * P:(t + 1) * P], tview(("OT", t), KD, P)))
            dve.wait_ge(late_in, 48)
            for t in range(T):
                done(dve, ("proj", t))
                emptied_by(("proj", t), dve.tensor_tensor(tok[:, t, :], place(("proj", t), D, P), tok[:, t, :], ALU.add))
                was_emptied(dve, ("proj", t))
                ins = dve.tensor_tensor(tok[:, t, :], tok[:, t, :], bp_row, ALU.add)
            link(ins)
            variance(5, tok, D)
            for t in range(T):
                normal(n2[:, t, :], tok[:, t, :], t).then_inc(ln_done["n2"], 1)
            for t in range(T):
                affine_T("h2T", t, h2T, 2)
            done(dve, ("gate",))
            emptied_by(("gate",), dve.tensor_copy(lg, v3(place(("gate",), T * E, P), T)))
            was_emptied(dve, ("gate",))
            def by_token(ap):
                return bass.AP(tensor=ap.tensor, offset=ap.offset, ap=[ap.ap[0], [1, T], [0, E]])
            link(dve.tensor_reduce(tmx, lg, AX_X, ALU.max))
            link(dve.tensor_tensor(sel, lg, by_token(tmx), ALU.is_equal))
            link(dve.tensor_tensor(sel, sel, spread(desc8, (P, T, E), 2), ALU.mult))
            link(dve.tensor_reduce(tmx, sel, AX_X, ALU.max))
            dve.tensor_tensor(sel, sel, by_token(tmx), ALU.is_equal).then_inc(sel_ok, 1)
            done(dve, ("rank",))
            emptied_by(("rank",), dve.tensor_copy(cum, v3(place(("rank",), (T + 1) * E, P), T + 1)))
            was_emptied(dve, ("rank",))
            number = cum[:, T, :]
            link(dve.tensor_scalar(nblk, number, 0.0, None, ALU.is_gt))
            for q in range(1, T):
                link(dve.scalar_tensor_tensor(out=nblk, in0=number, scalar=float(q * BR), in1=nblk,
                                              op0=ALU.is_gt, op1=ALU.add))
            link(dve.tensor_scalar(active, nblk, 0.0, None, ALU.is_gt))
            link(dve.tensor_tensor_scan(nblk_sum, nblk, zero8, 0.0, ALU.add, ALU.add))
            link(dve.tensor_tensor_scan(active_sum, active, zero8, 0.0, ALU.add, ALU.add))
            link(dve.tensor_tensor(start, nblk_sum, nblk, ALU.subtract))
            link(dve.tensor_tensor(order, active_sum, active, ALU.subtract))
            link(dve.tensor_scalar(base8, start, float(BR), None, ALU.mult))
            for t in range(T):
                link(dve.tensor_tensor(cum[:, t, :], cum[:, t, :], base8, ALU.add))
                link(dve.tensor_tensor_reduce(junk8, cum[:, t, :], sel[:, t, :], 1.0, 0.0, ALU.mult, ALU.add,
                                              pos_f[:, t:t + 1]))
            link(dve.tensor_copy(pos_i, pos_f))
            link(dve.tensor_tensor(match, spread(order, (1, E, E), 2), spread(iota8, (1, E, E), 1), ALU.is_equal))
            link(dve.tensor_tensor(match, match, spread(active, (1, E, E), 2), ALU.mult))
            for q, what in enumerate((iota8, nblk, start)):
                link(dve.tensor_tensor(prod, match, spread(what, (1, E, E), 2), ALU.mult))
                link(dve.tensor_reduce(tab_f[:, q, :], prod, AX_X, ALU.add))
            link(dve.tensor_copy(tab, tab_f))
            link(dve.tensor_copy(nblocks, nblk_sum[0:1, E - 1:E]))
            dve.tensor_copy(nact, active_sum[0:1, E - 1:E]).then_inc(routed, 1)
            done(dve, ("selT",))
            emptied_by(("selT",), dve.tensor_copy(v3(selT, T), tview(("selT",), T, P, E)))
            for t in range(T):
                done(dve, ("b2sum", t))
                emptied_by(("b2sum", t), dve.tensor_tensor(total[:, t, :], place(("b2sum", t), D, P), total[:, t, :], ALU.add))
                was_emptied(dve, ("b2sum", t))
                ins = dve.tensor_tensor(total[:, t, :], total[:, t, :], tok[:, t, :], ALU.add)
            link(ins)
            dve.sem_inc(final, 1)
            n_active = dve.value_load(nact[0:1, 0:1], min_val=1, max_val=E)
            dve.sem_inc(hid_relu, 2)
            dve.sem_inc(ht_ok, 1)
            with dve.Fori(0, n_active) as a:
                e = dve.value_load(tab[0:1, 0, bass.ds(a, 1)], min_val=0, max_val=E - 1)
                nb = dve.value_load(tab[0:1, 1, bass.ds(a, 1)], min_val=1, max_val=T)
                first = dve.value_load(tab[0:1, 2, bass.ds(a, 1)], min_val=0, max_val=NB - 1)
                with dve.Fori(0, nb) as i:
                    b = first + i
                    dve.wait_ge(xt_used, b + 1)
                    dve.wait_ge(hid_mm, b * C + C)
                    for k in range(KD):
                        ins = dve.tensor_scalar(ht[:, k, :], psum[:, 6 * BANK + k * BR:6 * BANK + (k + 1) * BR],
                                                cols[:, 2, k:k + 1], cols[:, 3, k:k + 1], ALU.mult, ALU.add)
                    ins.then_inc(ht_ok, 1)
                    for c in range(C):
                        dve.wait_ge(hid_tr, b * C + (c + 3))
                        dve.wait_ge(hid_used, b * C + (C + c - 1))
                        for j in range(CK):
                            ins = dve.tensor_scalar(
                                hidT[c % 2][:, j, :], psum[:, (2 + c % 2) * BANK + j * BR:(2 + c % 2) * BANK + (j + 1) * BR],
                                b1T[:, bass.ds(e * (C * CK) + (c * CK + j), 1)], 0.0, ALU.add, ALU.max)
                        ins.then_inc(hid_relu, 1)
            for t in range(T):
                dve.wait_ge(gathered[t], 16)
                dve.tensor_tensor(total[:, t, :], total[:, t, :], back[t], ALU.add).then_inc(final, 1)

        @block.tensor
        def _(pe):
            def turn(name, k, tile):
                free(pe, name)
                w = tile.shape[-1] // k
                parts = tile.shape[0]
                for q in range(k):
                    ins = pe.transpose(place(name)[0:w, q * 128:q * 128 + parts], tile[:, q * w:(q + 1) * w],
                                       ident[0:parts, 0:parts])
                ins.then_inc(made, 1)

            def product(name, k, left, right, width, parts):
                free(pe, name)
                at = 0
                while at < width:
                    w = min(BANK, width - at)
                    for q in range(k):
                        ins = pe.matmul(place(name)[0:parts, at:at + w], left(q), right(q)[:, at:at + w],
                                        start=(q == 0), stop=(q == k - 1))
                    at += w
                ins.then_inc(made, 1)

            pe.wait_ge(bounds_v, 1)
            out_e = place(("edges",))
            for a in range(2):
                for j in range(J):
                    pe.transpose(out_e[0:P, (a * J + j) * G:(a * J + j + 1) * G], edge_f[:, a, P * j:P * j + P],
                                 ident[0:G, 0:G])
            pe.transpose(out_e[0:2 * T, BANK:BANK + G], v_b, ident[0:G, 0:G]).then_inc(made, 1)
            pe.wait_ge(bounds_v, 2)
            pe.transpose(place(("bounds",))[0:1, 0:2 * T], vm, ident[0:2 * T, 0:2 * T]).then_inc(made, 1)

            for t in range(T):
                pe.wait_ge(ln_done["x0"], t + 1)
                turn(("x0T", t), KD, tok[:, t, :])
            pe.wait_ge(w1g_in, 16)
            was_emptied(pe, ("x0T", T - 1))
            was_emptied(pe, ("x0T", T - 2))
            for t in range(T):
                product(("xl1", t), KD, lambda k: aT6[:, k, t * P:(t + 1) * P], lambda k: w1_g[:, k, :], HC, P)
            pe.wait_ge(wr1g_in, 16)
            for t in range(T):
                product(("res1", t), KD, lambda k: aT6[:, k, t * P:(t + 1) * P], lambda k: wr1_g[:, k, :], HC, P)
            pe.wait_ge(bounds_r, 1)
            for d in range(T):
                groups = pe.value_load(ri[0:1, 2 * d:2 * d + 1], min_val=1, max_val=G)
                free(pe, ("count", d))
                pe.sem_inc(oh_used[d], J)
                low_, high = place(("count", d))[0:P, 0:BANK], place(("count", d))[0:P, BANK:N]
                pe.matmul(low_, zero16[:, 0:P], zero16[:, 0:BANK], start=True, stop=False)
                pe.matmul(high, zero16[:, 0:P], zero16[:, 0:N - BANK], start=True, stop=False)
                with pe.Fori(0, groups) as i:
                    for j in range(J):
                        pe.wait_ge(oh_ready[d], i * J + j + 1)
                        pe.matmul(low_, oh_dst[:, j, :], oh_src[:, j, 0:BANK], start=False, stop=False)
                        pe.matmul(high, oh_dst[:, j, :], oh_src[:, j, BANK:N], start=False,
                                  stop=False).then_inc(oh_used[d], 1)
                pe.matmul(low_, zero16[:, 0:P], zero16[:, 0:BANK], start=False, stop=True)
                pe.matmul(high, zero16[:, 0:P], zero16[:, 0:N - BANK], start=False, stop=True).then_inc(made, 1)

            def graph_attention(layer, heads, width, xl):
                n_, before_ = heads * T, 0 if layer == 1 else HEADS * T
                for i in range(n_ + 2):
                    if i < n_ and i % T == 0:
                        name = ("src_row", layer, i // T)
                        free(pe, name)
                        pe.wait_ge(row_ok, i // T + 1 + (HEADS if layer == 2 else 0))
                        for c0, c1 in [(t * P, (t + 1) * P) for t in range(T - 1)] + [(N - P, BANK), (BANK, N)]:
                            ins = pe.matmul(place(name)[0:P, c0:c1], ones[0:P, 0:P],
                                            low[0:P, TW + XW + CWD + c0:TW + XW + CWD + c1], start=True, stop=True)
                        ins.then_inc(made, 1)
                    if 1 <= i <= n_:
                        pe.wait_ge(prob_ok, before_ + i)
                        turn(("probT", layer, i - 1), T, zbuf[(before_ + i - 1) % 4])
                    if i >= 2:
                        h = (i - 2) // T
                        was_emptied(pe, ("probT", layer, i - 2))
                        product(("agg", layer, i - 2), T, lambda k: probT[i % 2][:, k, :],
                                lambda k: xl[:, k, h * width:(h + 1) * width], width, P)

            graph_attention(1, HEADS, HID, xl1)
            for t in range(T):
                pe.wait_ge(epi_c, t + 1)
                turn(("h1T", t), KH, res1[:, t, :])
            pe.wait_ge(w2g_in, 16)
            was_emptied(pe, ("h1T", T - 1))
            was_emptied(pe, ("h1T", T - 2))
            for t in range(T):
                product(("xl2", t), KH, lambda k: aT8[:, k, t * P:(t + 1) * P], lambda k: w2_g[:, k, :], D, P)
            pe.wait_ge(wr2g_in, 16)
            for t in range(T):
                product(("res2", t), KH, lambda k: aT8[:, k, t * P:(t + 1) * P], lambda k: wr2_g[:, k, :], D, P)
            graph_attention(2, 1, D, xl2)
            for t in range(T):
                pe.wait_ge(ln_done["n1"], t + 1)
                turn(("hT", t), KD, agg2[:, t, :])
            pe.wait_ge(wq_in, 16 * KD)
            was_emptied(pe, ("hT", T - 1))
            was_emptied(pe, ("hT", T - 2))
            for c in range(FC):
                product(("QT", c), KD, lambda k: wq_s[:, k, c * 128:(c + 1) * 128], lambda k: aT6[:, k, :], N, 128)
            pe.wait_ge(wk_in, 16 * KD)
            for c in range(FC):
                product(("KT", c), KD, lambda k: wk_s[:, k, c * 128:(c + 1) * 128], lambda k: aT6[:, k, :], N, 128)
            pe.wait_ge(wv_in, 16 * KD)
            for t in range(T):
                product(("V", t), KD, lambda k: aT6[:, k, t * P:(t + 1) * P], lambda k: wv_s[:, k, :], D, P)
            was_emptied(pe, ("QT", FC - 1))
            was_emptied(pe, ("KT", FC - 1))
            n_ = T * FH
            for i in range(n_ + 2):
                if i < n_:
                    t, h = divmod(i, FH)
                    half_ = slice(64 * (h % 2), 64 * (h % 2) + 64)
                    product(("score", i), 1, lambda k: QT[half_, h // 2, t * P:(t + 1) * P],
                            lambda k: KT[half_, h // 2, :], (t + 1) * P, P)
                if 1 <= i <= n_:
                    t = (i - 1) // FH
                    pe.wait_ge(sc_exp, i)
                    turn(("attT", i - 1), t + 1, abuf[(i - 1) % 3][:, 0:(t + 1) * P])
                if i >= 2:
                    t, h = divmod(i - 2, FH)
                    if i == 2:
                        was_emptied(pe, ("V", T - 1))
                    was_emptied(pe, ("attT", i - 2))
                    product(("pv", i - 2), t + 1, lambda k: attT[i % 2][:, k, :],
                            lambda k: Vt[:, k, h * HS:(h + 1) * HS], HS, P)
            was_emptied(pe, ("pv", n_ - 1))
            for t in range(T):
                turn(("OT", t), KD, O[:, t, :])
            pe.wait_ge(wp_in, 16)
            was_emptied(pe, ("OT", T - 1))
            was_emptied(pe, ("OT", T - 2))
            for t in range(T):
                product(("proj", t), KD, lambda k: aT6[:, k, t * P:(t + 1) * P], lambda k: wp_s[:, k, :], D, P)
            pe.wait_ge(late_in, 48)
            turn(("b1T",), 2, b1_rows)
            for t in range(T):
                pe.wait_ge(ln_done["n2"], t + 1)
                turn(("h2T", t), KD, n2[:, t, :])
            pe.wait_ge(small_in, 80)
            was_emptied(pe, ("h2T", T - 1))
            was_emptied(pe, ("h2T", T - 2))
            free(pe, ("gate",))
            for t in range(T):
                for k in range(KD):
                    ins = pe.matmul(place(("gate",))[0:P, t * E:(t + 1) * E], h2T[:, k, t * P:(t + 1) * P],
                                    wg_s[:, k, :], start=(k == 0), stop=(k == KD - 1))
            ins.then_inc(made, 1)
            pe.wait_ge(sel_ok, 1)
            free(pe, ("rank",))
            for t in range(T + 1):
                for q in range(min(t + 1, T)):
                    ins = pe.matmul(place(("rank",))[0:P, t * E:(t + 1) * E],
                                    before if q == t else ones[0:P, 0:P], sel[:, q, :],
                                    start=(q == 0), stop=(q == min(t, T - 1)))
            ins.then_inc(made, 1)
            free(pe, ("selT",))
            for t in range(T):
                ins = pe.transpose(place(("selT",))[0:E, t * 128:t * 128 + P], sel[:, t, :], ident[0:P, 0:P])
            ins.then_inc(made, 1)
            was_emptied(pe, ("selT",))
            for t in range(T):
                product(("b2sum", t), 1, lambda k: selT[:, t * P:(t + 1) * P], lambda k: b2_s, D, P)
            was_emptied(pe, ("b2sum", T - 1))

            pe.wait_ge(routed, 1)
            n_active = pe.value_load(nact[0:1, 0:1], min_val=1, max_val=E)
            pe.sem_inc(hid_tr, 2)
            pe.sem_inc(hid_mm, C)
            pe.sem_inc(hid_used, C)
            with pe.Fori(0, n_active) as a:
                nb = pe.value_load(tab[0:1, 1, bass.ds(a, 1)], min_val=1, max_val=T)
                first = pe.value_load(tab[0:1, 2, bass.ds(a, 1)], min_val=0, max_val=NB - 1)
                with pe.Fori(0, nb) as i:
                    b = first + i
                    pe.wait_ge(xt_in, b * 16 + 16)
                    pe.wait_ge(ht_ok, b + 1)
                    for k in range(KD):
                        ins = pe.transpose(psum[:, 6 * BANK + k * BR:6 * BANK + (k + 1) * BR],
                                           xt[:, k * 128:(k + 1) * 128], ident)
                    ins.then_inc(xt_used, 1)
                    pe.wait_ge(ht_ok, b + 2)

                    def first_product(c):
                        pe.wait_ge(w1_in[c], a * 16 + 16)
                        pe.wait_ge(hid_cp, b * C + (c + 1))
                        for k in range(KD):
                            ins = pe.matmul(psum[:, (c % 2) * BANK:(c % 2 + 1) * BANK], ht[:, k, :], w1_s[c][:, k, :],
                                            start=(k == 0), stop=(k == KD - 1))
                        ins.then_inc(hid_mm, 1)

                    first_product(0)
                    for c in range(C):
                        if c + 1 < C:
                            first_product(c + 1)
                        pe.wait_ge(hid_cp, b * C + (c + 3))
                        pe.wait_ge(hid_relu, b * C + (c + 1))
                        for j in range(CK):
                            ins = pe.transpose(psum[:, (2 + c % 2) * BANK + j * BR:(2 + c % 2) * BANK + (j + 1) * BR],
                                               hid[c % 2][:, j * 128:(j + 1) * 128], ident)
                        ins.then_inc(hid_tr, 1)
                        pe.wait_ge(w2_in[c], a * 16 + 16)
                        pe.wait_ge(hid_relu, b * C + (c + 3))
                        if c == 0:
                            pe.wait_ge(y_cp, b + 1)
                        for j in range(CK):
                            for q in range(2):
                                ins = pe.matmul(psum[:, (4 + q) * BANK:(4 + q) * BANK + D // 2], hidT[c % 2][:, j, :],
                                                w2_s[c][:, j, q * D // 2:(q + 1) * D // 2],
                                                start=(c == 0 and j == 0), stop=(c == C - 1 and j == CK - 1))
                        ins.then_inc(hid_used, 1)


_INS = ['x', 'src', 'dst', 'L0_gnn_W1', 'L0_gnn_a_src1', 'L0_gnn_a_dst1', 'L0_gnn_b1', 'L0_gnn_g1', 'L0_gnn_be1',
        'L0_gnn_Wr1', 'L0_gnn_br1', 'L0_gnn_W2', 'L0_gnn_a_src2', 'L0_gnn_a_dst2', 'L0_gnn_b2', 'L0_gnn_g2',
        'L0_gnn_be2', 'L0_gnn_Wr2', 'L0_gnn_br2', 'L0_ffn_ln1_g', 'L0_ffn_ln1_b', 'L0_ffn_ln2_g', 'L0_ffn_ln2_b',
        'L0_ffn_Wq', 'L0_ffn_Wk', 'L0_ffn_Wv', 'L0_ffn_Wp', 'L0_ffn_bp', 'L0_ffn_Wg', 'L0_ffn_W1', 'L0_ffn_b1',
        'L0_ffn_W2', 'L0_ffn_b2']
_OUTS = [((625, 768), 'float32')]


def kernel(**inputs):
    import numpy as _np
    import concourse.bacc as _bacc
    from concourse import mybir as _mybir
    from concourse.bass_utils import run_bass_kernel_spmd as _run

    nc = _bacc.Bacc("TRN2", target_bir_lowering=False, num_devices=1)
    arrays, args = {}, []
    for name in _INS:
        a = _np.ascontiguousarray(inputs[name])
        arrays[f"in_{name}_dram"] = a
        args.append(nc.dram_tensor(f"in_{name}_dram", a.shape, _mybir.dt.from_np(a.dtype), kind="ExternalInput").ap())
    for i, (shape, dtype) in enumerate(_OUTS):
        dt = _mybir.dt.from_np(_np.dtype(dtype))
        args.append(nc.dram_tensor(f"out_{i}_dram", shape, dt, kind="ExternalOutput").ap())
    gnn_moe_kernel(nc, *args)
    r = _run(nc, [arrays], core_ids=[0])
    got = tuple(r.results[0][f"out_{i}_dram"] for i in range(len(_OUTS)))
    return got[0]
```

```python
from contextlib import ExitStack

import concourse.bass as bass
from concourse import mybir

F32, F16, I32, U32 = mybir.dt.float32, mybir.dt.float16, mybir.dt.int32, mybir.dt.uint32
ACT = mybir.ActivationFunctionType
ALU = mybir.AluOpType
AX_X = mybir.AxisListType.X
BIG = 1e30
BANK = 512
SLOT = 2 * BANK
SLOTS = 4


def item_plan(T, HEADS, FH, FC):
    plan = [(("edges",), "D"), (("bounds",), "D")]
    plan += [(("x0T", t), "AD"[t % 2]) for t in range(T)]
    plan += [(("xl1", t), "A") for t in range(T)]
    plan += [(("res1", t), "D") for t in range(T)]
    plan += [(("count", t), "D") for t in range(T)]
    for layer, heads in ((1, HEADS), (2, 1)):
        if layer == 2:
            plan += [(("h1T", t), "AD"[t % 2]) for t in range(T)]
            plan += [(("xl2", t), "A") for t in range(T)]
            plan += [(("res2", t), "D") for t in range(T)]
        n = heads * T
        for i in range(n + 2):
            if i < n and i % T == 0:
                plan.append((("src_row", layer, i // T), "A"))
            if 1 <= i <= n:
                plan.append((("probT", layer, i - 1), "A"))
            if i >= 2:
                plan.append((("agg", layer, i - 2), "D"))
    plan += [(("hT", t), "AD"[t % 2]) for t in range(T)]
    plan += [(("QT", c), "A") for c in range(FC)] + [(("KT", c), "D") for c in range(FC)]
    plan += [(("V", t), "A") for t in range(T)]
    n = T * FH
    for i in range(n + 2):
        if i < n:
            plan.append((("score", i), "D"))
        if 1 <= i <= n:
            plan.append((("attT", i - 1), "A"))
        if i >= 2:
            plan.append((("pv", i - 2), "D"))
    plan += [(("OT", t), "AD"[t % 2]) for t in range(T)]
    plan += [(("proj", t), "D") for t in range(T)]
    plan += [(("b1T",), "A")]
    plan += [(("h2T", t), "AD"[t % 2]) for t in range(T)]
    plan += [(("gate",), "D"), (("rank",), "D"), (("selT",), "D")]
    plan += [(("b2sum", t), "D") for t in range(T)]
    return plan


def gnn_moe_kernel(nc, x, src, dst, g_W1, g_as1, g_ad1, g_b1, g_g1, g_be1, g_Wr1, g_br1, g_W2, g_as2, g_ad2,
                   g_b2, g_g2, g_be2, g_Wr2, g_br2, ln1_g, ln1_b, ln2_g, ln2_b, Wq, Wk, Wv, Wp, bp, Wg,
                   W1, b1, W2, b2, out):
    N, D = x.shape
    NE = src.shape[0]
    P = 125
    T = N // P
    HEADS, HID = g_as1.shape
    HC = HEADS * HID
    FH, _, HS = Wq.shape
    E, _, DF = W1.shape
    KD, KH = D // 128, HC // 128
    FC = FH * HS // 128
    G, J = 40, NE // (40 * P)
    assert T * P == N and G * J * P == NE and FC * 128 == FH * HS and HS == 64
    SCALE = float(D) ** -0.5
    EPS = 1e-5
    C, CW = 6, DF // 6
    CK = CW // 128
    assert CW == BANK and C % 2 == 0
    BR = 128
    NB = T + E - 1
    assert BR * T >= N

    plan = item_plan(T, HEADS, FH, FC)
    item = {name: n for n, (name, _) in enumerate(plan)}
    emptied = []
    for n, (_, who) in enumerate(plan):
        emptied.append((who, sum(w == who for _, w in plan[:n + 1])))

    hs_dram = nc.dram_tensor("sorted_tokens", [(NB + 2) * BR, D], F32, kind="Internal").ap()
    ys_dram = nc.dram_tensor("sorted_results", [(NB + 2) * BR, D], F32, kind="Internal").ap()

    with ExitStack() as ctx:
        def sem(name):
            return ctx.enter_context(nc.semaphore(name))

        SW = 6144
        area = ctx.enter_context(nc.sbuf_tensor("area", [128, 6 * SW], F32))
        TW, XW, CWD = KH * N, T * D, T * N
        low = ctx.enter_context(nc.sbuf_tensor("low", [128, TW + 2 * XW + CWD], F32))
        psum = ctx.enter_context(nc.psum_tensor("psum", [128, SLOTS * SLOT], F32))

        def A(slot, at, n, parts=128):
            return area[0:parts, slot * SW + at:slot * SW + at + n]

        def v3(ap, a):
            return ap.rearrange("p (a b) -> p a b", a=a)

        T_ = low[:, 0:TW]
        X_ = low[0:P, TW:TW + XW]
        S_ = low[0:P, TW + XW:TW + 2 * XW]
        C_ = low[0:P, TW + 2 * XW:TW + 2 * XW + CWD]
        aT6, aT8 = v3(T_[:, 0:KD * N], KD), v3(T_, KH)
        tok = v3(X_, T)
        total = v3(S_, T)
        counts = v3(C_, T)
        absent = v3(low[0:P, TW + XW:TW + XW + CWD], T)
        zbuf = [low[0:P, TW + i * N:TW + (i + 1) * N] for i in range(4)]
        x_again = v3(low[0:P, 0:XW], T)

        w1_g, wr1_g = v3(A(0, 0, KD * HC), KD), v3(A(1, 0, KD * HC), KD)
        w2_g, wr2_g = v3(A(0, 0, KH * D), KH), v3(A(1, 0, KH * D), KH)
        row_a = [A(2, 0, HC, P), A(2, HC, HC, P)]
        oh_src = v3(A(2, 2048, J * 626 // 2, P).bitcast(F16), J)[:, :, 0:N]
        oh_dst = v3(A(2, 3300, J * 128 // 2, P).bitcast(F16), J)[:, :, 0:P]
        iota16 = A(2, 3556, 313, P).bitcast(F16)
        zero16 = A(2, 3869, BANK // 2).bitcast(F16)
        edge_i = v3(A(2, 4125, 2 * J * P, G).bitcast(I32), 2)
        edge_f = v3(A(2, 5125, 2 * J * P, G), 2)
        agg1 = v3(A(2, 0, T * HC, P), T)
        agg2 = v3(A(2, 0, T * D, P), T)
        row1 = {n: A(3, i * HC, HC, P) for i, n in enumerate(("br1", "b1", "g1", "be1"))}
        row2 = {n: A(3, i * D, D, P) for i, n in enumerate(("br2", "b2", "g2", "be2"))}
        probT = [v3(A(3, 4096 + i * N, N, P), T) for i in range(2)]
        eT = A(3, 4096 + 2 * N, 2 * J * 2 * G, P).rearrange("p (a j g) -> p a j g", a=2, j=J)
        xl1, xl2 = v3(A(4, 0, T * HC, P), T), v3(A(4, 0, T * D, P), T)
        src_row = [A(4, T * HC, N, P), A(5, T * HC, N, P)]
        res1, res2 = v3(A(5, 0, T * HC, P), T), v3(A(5, 0, T * D, P), T)
        row_a2 = [A(2, 4096, D, P), A(2, 4096 + D, D, P)]
        wq_s, wk_s, wv_s, wp_s = (v3(A(s, 0, KD * D), KD) for s in (0, 1, 4, 1))
        QT, KT = v3(A(5, 0, FC * N), FC), v3(A(3, 0, FC * N), FC)
        Vt, O = v3(A(2, 0, T * D, P), T), v3(A(0, 0, T * D, P), T)
        causal = A(3, FC * N, N, P)
        bp_row = A(3, FC * N + N, D, P)
        abuf = [low[0:P, TW + 2 * XW + i * N:TW + 2 * XW + (i + 1) * N] for i in range(3)]
        attT = [v3(low[0:P, TW + 2 * XW + (3 + i) * N:TW + 2 * XW + (4 + i) * N], T) for i in range(2)]
        n2 = v3(A(5, 0, T * D, P), T)
        h2T = v3(A(4, 0, KD * N), KD)
        b2_s = A(2, 4096, D, E)
        b1_rows = A(2, 4096 + D, 2 * 128, 96)
        W1W, W2W = KD * CW // 2, CK * D // 2
        w1_s = [[v3(A(c, q * W1W, W1W).bitcast(F16), KD) for q in range(2)] for c in range(C)]
        w2_s = [[v3(A(c, 2 * W1W + q * W2W, W2W).bitcast(F16), CK) for q in range(2)] for c in range(C)]
        RING = 4
        raw = [low[:, at:at + W1W] for at in (TW, TW + W1W, TW + 2 * XW, TW + 2 * XW + W1W)]
        assert W1W == W2W and 2 * W1W + D <= XW and 2 * W1W <= CWD
        y_o = low[:, TW + 2 * W1W:TW + 2 * W1W + D]
        xt = T_[:, 0:D]
        turned = v3(xt, KD)
        at_t = [D]

        def carve(n):
            at_t[0] += n
            assert at_t[0] <= 4400
            return T_[:, at_t[0] - n:at_t[0]]

        ht = [v3(carve(D // 2).bitcast(F16), KD) for _ in range(2)]
        hid = [carve(CW) for _ in range(2)]
        relu = carve(CW)
        hidT = [[v3(carve(CW // 2).bitcast(F16), CK) for _ in range(2)] for _ in range(2)]
        UNITS = [(w, c, q) for s in range(1, C + 2) for w, c in ((1, s - 1), (2, s - 2)) if 0 <= c < C
                 for q in range(2)]
        U = len(UNITS)
        unit_of = {key: u for u, key in enumerate(UNITS)}
        assert U % RING == 0
        back = [low[0:P, TW + 2 * XW + q * D:TW + 2 * XW + (q + 1) * D] for q in range(4)] + [X_[:, 0:D]]

        def unit_parts(u):
            w, c, q = UNITS[u]
            n = (KD if w == 1 else CK) // 2
            return [part[:, q * n:(q + 1) * n, :] for part in (w1_s if w == 1 else w2_s)[c]]

        def raw_view(u):
            return v3(raw[u % RING], (KD if UNITS[u][0] == 1 else CK) // 2)

        smalls = ctx.enter_context(nc.sbuf_tensor("smalls", [128, 528], F32))
        carved = [0]

        def small(parts, *shape, dt=F32):
            n = 1
            for k in shape:
                n *= k
            v = smalls[0:parts, carved[0]:carved[0] + n]
            carved[0] += n
            assert carved[0] <= 528
            if dt is not F32:
                v = v.bitcast(dt)
            return v3(v, shape[0]) if len(shape) == 2 else v

        ident, ones = small(128, 128), small(128, 128)
        stats, mv = small(P, T, 12), small(P, T, 2)
        rstd, half = small(P, T), small(P, T)
        a_src, a_dst = small(P, T, HEADS), small(P, T, HEADS)
        negm, rsum, rinv = small(P, 4), small(P, 4), small(P, 4)
        cols = small(128, 4, KD)
        wg_s = small(128, KD, E)
        pos_i = small(P, T, dt=U32)
        tab = small(1, 4, NB, dt=I32)
        nblocks = small(1, 1, dt=I32)
        at3 = 4096 + 2 * N + 4 * J * G
        g_i, mm_s, v_b = A(3, at3, 2, G), A(3, at3 + 2, 2, G), A(3, at3 + 4, 2 * T, G)
        h_a, h_b = A(3, at3 + 14, 1, G), A(3, at3 + 15, 1, G)
        vm, rr, ri = A(3, at3 + 16, 1, 2 * T), A(3, at3 + 17, 2 * T, 1), A(3, at3 + 27, 2 * T, 1).bitcast(I32)
        assert at3 + 40 <= SW
        at2 = [5120]

        def scratch(parts, *shape):
            n = shape[0] * (shape[1] if len(shape) == 2 else 1)
            v = A(2, at2[0], n, parts)
            at2[0] += n
            assert at2[0] <= SW
            return v3(v, shape[0]) if len(shape) == 2 else v

        lg, sel, cum = scratch(P, T, E), scratch(P, T, E), scratch(P, T + 1, E)
        tmx, pos_f = scratch(P, T), scratch(P, T)
        iota8, desc8, zero8 = scratch(P, E), scratch(P, E), scratch(P, E)
        nblk, nblk_sum, start, active, active_sum, order, base8, junk8 = (scratch(P, E) for _ in range(8))
        block_no, match, prod, tab_f = scratch(1, NB), scratch(1, NB, E), scratch(1, NB, E), scratch(1, 4, NB)
        before = A(3, FC * N + N + D, P, P)
        selT = A(2, 0, N, E)
        b1T = T_[:, 4400:4400 + E * DF // 128]

        x_in, edges_in, rows1_in, rows2_in = sem("x_in"), sem("edges_in"), sem("rows1_in"), sem("rows2_in")
        arows1_in, arows2_in, x2_in, small_in = sem("arows1_in"), sem("arows2_in"), sem("x2_in"), sem("small_in")
        w1g_in, wr1g_in, w2g_in, wr2g_in = sem("w1g_in"), sem("wr1g_in"), sem("w2g_in"), sem("wr2g_in")
        wq_in, wk_in, wv_in, wp_in, late_in = sem("wq_in"), sem("wk_in"), sem("wv_in"), sem("wp_in"), sem("late_in")
        consts = sem("consts")
        made = sem("made")
        act_emptied, dve_emptied = sem("act_emptied"), sem("dve_emptied")
        step = sem("step")
        pstep = sem("pstep")
        bounds_v, bounds_r, edge_ready = sem("bounds_v"), sem("bounds_r"), sem("edge_ready")
        oh_ready = [sem(f"oh_ready{d}") for d in range(T)]
        oh_used = [sem(f"oh_used{d}") for d in range(T)]
        var_ok, rstd_ok = sem("var_ok"), sem("rstd_ok")
        ln_done = {n: sem(f"ln_{n}") for n in ("x0", "n1", "n2")}
        row_ok, pair_ok, neg_ok, exp_ok, prob_ok = (sem(n) for n in ("row_ok", "pair_ok", "neg_ok", "exp_ok", "prob_ok"))
        epi_a, epi_b, epi_c = sem("epi_a"), sem("epi_b"), sem("epi_c")
        sc_exp = sem("sc_exp")
        y1_ok, routed, padded, scattered = sem("y1_ok"), sem("routed"), sem("padded"), sem("scattered")
        raw_in = [sem(f"raw_in{q}") for q in range(RING)]
        high_ok, low_ok = sem("high_ok"), sem("low_ok")
        relu_ok, hthi_ok = sem("relu_ok"), sem("hthi_ok")
        turned_ok = sem("turned_ok")
        xt_in, xt_used, xtT, ht_ok = sem("xt_in"), sem("xt_used"), sem("xtT"), sem("ht_ok")
        hid_mm, hid_cp, hid_tr, hid_relu, hid_used = (sem(n) for n in ("hid_mm", "hid_cp", "hid_tr", "hid_relu", "hid_used"))
        hidhi_ok = sem("hidhi_ok")
        y_cp, y_out = sem("y_cp"), sem("y_out")
        gathered = [sem(f"gathered{t}") for t in range(T)]
        final, stored, sel_ok = sem("final"), sem("stored"), sem("sel_ok")
        all_stored = sem("all_stored")

        def place(name, n=SLOT, parts=128):
            s = item[name] % SLOTS
            return psum[0:parts, s * SLOT:s * SLOT + n]

        def free(pe, name):
            if item[name] >= SLOTS:
                who, n = emptied[item[name] - SLOTS]
                pe.wait_ge(act_emptied if who == "A" else dve_emptied, n)

        def done(eng, name):
            eng.wait_ge(made, item[name] + 1)

        def was_emptied(eng, name):
            who, n = emptied[item[name]]
            eng.wait_ge(act_emptied if who == "A" else dve_emptied, n)

        def tview(name, k, n, parts=128):
            return v3(place(name, k * 128, parts), k)[:, :, 0:n]

        def bcast(row, parts):
            return bass.AP(tensor=row.tensor, offset=row.offset, ap=[[0, parts], [1, row.shape[0]]])

        def spread(ap, shape, keep):
            steps = [[0, shape[1]], [0, shape[2]]]
            steps[keep - 1] = [1, shape[keep]]
            return bass.AP(tensor=ap.tensor, offset=ap.offset, ap=[[ap.ap[0][0], shape[0]], *steps])

        AHEAD = 3

        def group(convert, a, b, g):
            for w, c in ((1, g - 1), (2, g - 2)):
                if 0 <= c < C:
                    convert(a, b, w, c)

        def expert_blocks(eng, convert, first_tokens, block_steps):
            blocks = eng.value_load(nblocks[0:1, 0:1], min_val=1, max_val=NB)
            first_tokens(0)
            for g in range(1, AHEAD + 1):
                group(convert, 0, 0, g)
            with eng.Fori(0, blocks) as b:
                e = eng.value_load(tab[0:1, 0, bass.ds(b, 1)], min_val=0, max_val=E - 1)
                a = eng.value_load(tab[0:1, 1, bass.ds(b, 1)], min_val=0, max_val=E - 1)
                is_first = eng.value_load(tab[0:1, 2, bass.ds(b, 1)], min_val=0, max_val=1)
                new_next = eng.value_load(tab[0:1, 3, bass.ds(b, 1)], min_val=0, max_val=1)
                SPLIT = C - AHEAD + 2
                with eng.If(is_first > 0):
                    for s_ in range(SPLIT):
                        block_steps(b, e, s_)
                        if s_ >= 1:
                            group(convert, a, b, s_ + AHEAD)
                with eng.Else():
                    for s_ in range(SPLIT):
                        block_steps(b, e, s_)
                with eng.If(new_next > 0):
                    for s_ in range(SPLIT, C + 2):
                        block_steps(b, e, s_)
                        group(convert, a + 1, b + 1, s_ - SPLIT + 1)
                with eng.Else():
                    for s_ in range(SPLIT, C + 2):
                        block_steps(b, e, s_)

        block = ctx.enter_context(nc.Block())

        @block.sync
        def _(sp):
            sp.dma_start(edge_i[:, 0, :], src.rearrange("(g n) -> g n", g=G)).then_inc(edges_in, 16)
            sp.dma_start(edge_i[:, 1, :], dst.rearrange("(g n) -> g n", g=G)).then_inc(edges_in, 16)
            for t in range(T):
                sp.dma_start(tok[:, t, :], x[t * P:(t + 1) * P, :]).then_inc(x_in, 16)
            sp.dma_start(w1_g, g_W1.rearrange("(k p) n -> p k n", p=128)).then_inc(w1g_in, 16)
            sp.dma_start(wr1_g, g_Wr1.rearrange("(k p) n -> p k n", p=128)).then_inc(wr1g_in, 16)
            for r, a in zip(row_a, (g_as1, g_ad1)):
                sp.dma_start(r, bcast(a.rearrange("h c -> (h c)"), P)).then_inc(arows1_in, 16)
            for n, a in (("br1", g_br1), ("b1", g_b1), ("g1", g_g1), ("be1", g_be1)):
                sp.dma_start(row1[n], bcast(a, P)).then_inc(rows1_in, 16)
            for i, a in enumerate((ln1_g, ln1_b, ln2_g, ln2_b)):
                sp.dma_start(cols[:, i, :], a.rearrange("(k p) -> p k", p=128),
                             allow_slow_non_contiguous=True).then_inc(small_in, 16)
            sp.dma_start(wg_s[:, :, :], Wg.rearrange("(k p) e -> p k e", p=128)).then_inc(small_in, 16)
            done(sp, ("xl1", T - 1))
            sp.dma_start(w2_g, g_W2.rearrange("(k p) n -> p k n", p=128)).then_inc(w2g_in, 16)
            done(sp, ("res1", T - 1))
            sp.dma_start(wr2_g, g_Wr2.rearrange("(k p) n -> p k n", p=128)).then_inc(wr2g_in, 16)
            sp.wait_ge(epi_c, T)
            for n, a in (("br2", g_br2), ("b2", g_b2), ("g2", g_g2), ("be2", g_be2)):
                sp.dma_start(row2[n], bcast(a, P)).then_inc(rows2_in, 16)
            for r, a in zip(row_a2, (g_as2, g_ad2)):
                sp.dma_start(r, bcast(a.rearrange("h c -> (h c)"), P)).then_inc(arows2_in, 16)
            done(sp, ("xl2", T - 1))
            for k in range(KD):
                sp.dma_start(wq_s[:, k, :].rearrange("p (h s) -> p h s", h=FH),
                             Wq[:, k * 128:(k + 1) * 128, :].rearrange("h p s -> p h s")).then_inc(wq_in, 16)
            done(sp, ("res2", T - 1))
            sp.dma_start(x_again, x.rearrange("(t p) d -> p t d", p=P)).then_inc(x2_in, 16)
            for k in range(KD):
                sp.dma_start(wk_s[:, k, :].rearrange("p (h s) -> p h s", h=FH),
                             Wk[:, k * 128:(k + 1) * 128, :].rearrange("h p s -> p h s")).then_inc(wk_in, 16)
            done(sp, ("agg", 2, T - 1))
            for k in range(KD):
                sp.dma_start(wv_s[:, k, :].rearrange("p (h s) -> p h s", h=FH),
                             Wv[:, k * 128:(k + 1) * 128, :].rearrange("h p s -> p h s")).then_inc(wv_in, 16)
            done(sp, ("KT", FC - 1))
            sp.dma_start(wp_s, Wp.rearrange("(k p) n -> p k n", p=128)).then_inc(wp_in, 16)
            sp.dma_start(bp_row, bcast(bp, P)).then_inc(late_in, 16)
            sp.dma_start(b2_s, b2).then_inc(late_in, 16)
            sp.dma_start(v3(b1_rows, 2), b1.rearrange("e f -> (e f)").rearrange("(a r c) -> r a c", a=2, c=128)).then_inc(late_in, 16)
            sp.wait_ge(routed, 1)
            blocks = sp.value_load(nblocks[0:1, 0:1], min_val=1, max_val=NB)
            done(sp, ("b2sum", T - 1))
            sp.wait_ge(final, 1)
            with sp.Fori(0, blocks) as b:
                e = sp.value_load(tab[0:1, 0, bass.ds(b, 1)], min_val=0, max_val=E - 1)
                a = sp.value_load(tab[0:1, 1, bass.ds(b, 1)], min_val=0, max_val=E - 1)
                is_first = sp.value_load(tab[0:1, 2, bass.ds(b, 1)], min_val=0, max_val=1)
                with sp.If(is_first > 0):
                    for u, (w, c, q) in enumerate(UNITS):
                        sp.wait_ge(low_ok, a * U + (u + 1))
                        if w == 1:
                            half_chunk = W1[bass.ds(e, 1), q * D // 2:(q + 1) * D // 2, c * CW:(c + 1) * CW]
                        else:
                            half_chunk = W2[bass.ds(e, 1), c * CW + q * CW // 2:c * CW + (q + 1) * CW // 2, :]
                        sp.dma_start(raw_view(u), half_chunk.rearrange("a (k p) n -> p (a k) n", p=128))\
                            .then_inc(raw_in[u % RING], 16)
            for t in range(T):
                sp.wait_ge(final, t + 2)
                sp.dma_start(out[t * P:(t + 1) * P, :], total[:, t, :]).then_inc(stored, 16)
            sp.wait_ge(stored, 16 * T)

        @block.gpsimd
        def _(pool):
            n = [0]

            def link(ins):
                n[0] += 1
                ins.then_inc(pstep, 1)
                pool.wait_ge(pstep, n[0])

            link(pool.memset(ones, 0.0))
            link(pool.affine_select(out=ident, in_=ones, compare_op=ALU.not_equal, fill=1.0, base=0,
                                    pattern=[[-1, 128]], channel_multiplier=1))
            link(pool.memset(ones, 1.0))
            link(pool.memset(zero16, 0.0))
            link(pool.memset(half, -0.5))
            link(pool.iota(iota16[:, 0:N], pattern=[[1, N]], base=0, channel_multiplier=0,
                           allow_small_or_imprecise_dtypes=True))
            link(pool.iota(g_i[:, 0:1], pattern=[[1, 1]], base=1, channel_multiplier=1,
                           allow_small_or_imprecise_dtypes=True))
            pool.iota(g_i[:, 1:2], pattern=[[1, 1]], base=G, channel_multiplier=-1,
                      allow_small_or_imprecise_dtypes=True).then_inc(consts, 1)
            zeros = zero16.bitcast(F32)
            zsrc = bass.AP(tensor=zeros.tensor, offset=zeros.offset, ap=[[zeros.ap[0][0], 128], [0, NB + 2], [1, 256]])
            for rows in (hs_dram, ys_dram):
                for c in range(0, D, 256):
                    pool.dma_start(rows.rearrange("(q p) n -> p q n", p=BR)[:, :, c:c + 256],
                                   zsrc).then_inc(padded, 16)

            def inverse_root(k):
                pool.wait_ge(var_ok, k + 1)
                link(pool.tensor_scalar(rstd, mv[:, :, 1], EPS, None, ALU.add))
                pool.tensor_tensor(rstd, rstd, half, ALU.pow).then_inc(rstd_ok, 1)

            inverse_root(0)
            inverse_root(1)
            pool.wait_ge(rows1_in, 64)
            for t in range(T):
                pool.wait_ge(epi_a, t + 1)
                link(pool.tensor_tensor(agg1[:, t, :], agg1[:, t, :], row1["g1"], ALU.mult))
                pool.tensor_tensor(agg1[:, t, :], agg1[:, t, :], row1["be1"], ALU.add).then_inc(epi_b, 1)
            inverse_root(2)
            pool.wait_ge(rows2_in, 64)
            for t in range(T):
                pool.wait_ge(epi_a, T + t + 1)
                link(pool.tensor_tensor(agg2[:, t, :], agg2[:, t, :], row2["g2"], ALU.mult))
                link(pool.tensor_tensor(agg2[:, t, :], agg2[:, t, :], row2["be2"], ALU.add))
                pool.tensor_tensor(agg2[:, t, :], agg2[:, t, :], res2[:, t, :], ALU.add).then_inc(epi_b, 1)
            inverse_root(3)
            inverse_root(4)
            was_emptied(pool, ("hT", T - 1))
            was_emptied(pool, ("hT", T - 2))
            link(pool.memset(causal, 0.0))
            link(pool.affine_select(out=causal[:, N - P:N], in_=causal[:, N - P:N], compare_op=ALU.is_ge, fill=-BIG,
                                    base=0, pattern=[[-1, P]], channel_multiplier=1))
            link(pool.memset(before, 1.0))
            link(pool.affine_select(out=before, in_=before, compare_op=ALU.is_gt, fill=0.0,
                                    base=0, pattern=[[1, P]], channel_multiplier=-1))
            link(pool.memset(zero8, 0.0))
            link(pool.iota(block_no, pattern=[[1, NB]], base=0, channel_multiplier=0, allow_small_or_imprecise_dtypes=True))
            link(pool.iota(iota8, pattern=[[1, E]], base=0, channel_multiplier=0, allow_small_or_imprecise_dtypes=True))
            pool.iota(desc8, pattern=[[-1, E]], base=E, channel_multiplier=0,
                      allow_small_or_imprecise_dtypes=True).then_inc(consts, 1)
            inverse_root(5)
            pool.wait_ge(padded, 32 * (D // 256))
            pool.wait_ge(ln_done["n2"], T)
            pool.wait_ge(routed, 1)
            for t in range(T):
                pool.indirect_dma_start(hs_dram, bass.IndirectOffsetOnAxis(ap=pos_i[:, t:t + 1], axis=0),
                                        n2[:, t, :], None).then_inc(scattered, 16)
            pool.wait_ge(scattered, 16 * T)
            pool.wait_ge(all_stored, 1)
            pool.wait_ge(final, 1)
            for t in range(T):
                pool.indirect_dma_start(back[t], None, ys_dram,
                                        bass.IndirectOffsetOnAxis(ap=pos_i[:, t:t + 1], axis=0)).then_inc(gathered[t], 16)

        @block.scalar
        def _(act):
            last = [-1]

            def emptied_by(name, ins):
                assert plan[item[name]][1] == "A" and item[name] > last[0]
                last[0] = item[name]
                ins.then_inc(act_emptied, 1)

            def copy(name, dst, src):
                done(act, name)
                emptied_by(name, act.activation(dst, src, ACT.Copy))

            for t in range(T):
                if plan[item["x0T", t]][1] == "A":
                    copy(("x0T", t), aT6[:, :, t * P:(t + 1) * P], tview(("x0T", t), KD, P))
            for t in range(T):
                copy(("xl1", t), xl1[:, t, :], place(("xl1", t), HC, P))
            for layer, heads in ((1, HEADS), (2, 1)):
                if layer == 2:
                    for t in range(T):
                        if plan[item["h1T", t]][1] == "A":
                            copy(("h1T", t), aT8[:, :, t * P:(t + 1) * P], tview(("h1T", t), KH, P))
                    for t in range(T):
                        copy(("xl2", t), xl2[:, t, :], place(("xl2", t), D, P))
                n, before_ = heads * T, 0 if layer == 1 else HEADS * T
                for i in range(n + 2):
                    g = before_ + i
                    if i >= 2:
                        if i >= 4:
                            done(act, ("agg", layer, i - 4))
                        copy(("probT", layer, i - 2), probT[i % 2], tview(("probT", layer, i - 2), T, P, P))
                    if i < n:
                        h, t = divmod(i, T)
                        if t == 0:
                            copy(("src_row", layer, h), src_row[h % 2], place(("src_row", layer, h), N, P))
                            act.wait_ge(act_emptied, emptied[item["src_row", layer, h]][1])
                        if i >= 4:
                            done(act, ("probT", layer, i - 4))
                        act.activation(zbuf[g % 4], src_row[h % 2], ACT.Identity,
                                       bias=a_dst[:, t, h:h + 1]).then_inc(pair_ok, 1)
                    if 1 <= i <= n:
                        act.wait_ge(neg_ok, g)
                        act.activation(zbuf[(g - 1) % 4], zbuf[(g - 1) % 4], ACT.Exp, scale=-1.0,
                                       bias=negm[:, (g - 1) % 4:(g - 1) % 4 + 1]).then_inc(exp_ok, 1)
            for t in range(T):
                if plan[item["hT", t]][1] == "A":
                    done(act, ("hT", t))
                    for k in range(KD):
                        ins = act.activation(aT6[:, k, t * P:(t + 1) * P], tview(("hT", t), KD, P)[:, k, :],
                                             ACT.Identity, scale=cols[:, 0, k:k + 1], bias=cols[:, 1, k:k + 1])
                    emptied_by(("hT", t), ins)
            for c in range(FC):
                copy(("QT", c), QT[:, c, :], place(("QT", c), N))
            for t in range(T):
                copy(("V", t), Vt[:, t, :], place(("V", t), D, P))
            n = T * FH
            for i in range(n + 2):
                if i < n:
                    was_emptied(act, ("score", i))
                    if i >= 4:
                        act.wait_ge(dve_emptied, emptied[item["pv", i - 4]][1])
                    w = (i // FH + 1) * P
                    act.activation(abuf[i % 3][:, 0:w], abuf[i % 3][:, 0:w], ACT.Exp, scale=-1.0,
                                   bias=negm[:, i % 4:i % 4 + 1],
                                   accum_out=rsum[:, i % 4:i % 4 + 1]).then_inc(sc_exp, 1)
                if 1 <= i <= n:
                    if i >= 3:
                        done(act, ("pv", i - 3))
                    k = (i - 1) // FH + 1
                    copy(("attT", i - 1), attT[(i - 1) % 2][:, 0:k, :], tview(("attT", i - 1), k, P, P))
            for t in range(T):
                if plan[item["OT", t]][1] == "A":
                    copy(("OT", t), aT6[:, :, t * P:(t + 1) * P], tview(("OT", t), KD, P))
            done(act, ("proj", T - 1))
            copy(("b1T",), v3(b1T, 2), v3(place(("b1T",), 256), 2)[:, :, 0:96])
            for t in range(T):
                if plan[item["h2T", t]][1] == "A":
                    done(act, ("h2T", t))
                    for k in range(KD):
                        ins = act.activation(h2T[:, k, t * P:(t + 1) * P], tview(("h2T", t), KD, P)[:, k, :],
                                             ACT.Identity, scale=cols[:, 2, k:k + 1], bias=cols[:, 3, k:k + 1])
                    emptied_by(("h2T", t), ins)
            act.wait_ge(routed, 1)
            was_emptied(act, ("b2sum", T - 1))
            act.sem_inc(hid_cp, 2)
            act.sem_inc(y_cp, 1)

            def high_parts(a, b, w, c):
                if c == C - 1:
                    act.wait_ge(scattered, 16 * T)
                for q in range(2):
                    u = unit_of[w, c, q]
                    act.wait_ge(raw_in[u % RING], a * (U // RING * 16) + (u // RING + 1) * 16)
                    act.wait_ge(hid_mm if w == 1 else hid_used, b * C + (c + 1))
                    act.activation(unit_parts(u)[0], raw_view(u), ACT.Copy).then_inc(high_ok, 1)

            def tokens_high(b):
                act.wait_ge(turned_ok, b + 1)
                act.wait_ge(hid_mm, b * C + C)
                act.activation(ht[0], turned, ACT.Copy).then_inc(hthi_ok, 1)

            def block_steps(b, e, s_):
                if s_ < C:
                    act.wait_ge(hid_mm, b * C + (C + s_ + 1))
                    act.wait_ge(hid_tr, b * C + (s_ + 1))
                    act.activation(hid[s_ % 2], psum[:, (s_ % 2) * BANK:(s_ % 2 + 1) * BANK],
                                   ACT.Copy).then_inc(hid_cp, 1)
                if s_ == C:
                    tokens_high(b + 1)
                if 1 <= s_ <= C:
                    c = s_ - 1
                    act.wait_ge(relu_ok, b * C + (c + 1))
                    act.wait_ge(hid_used, b * C + (C + c - 1))
                    act.activation(hidT[c % 2][0], v3(relu, CK), ACT.Copy).then_inc(hidhi_ok, 1)
                if s_ == C + 1:
                    act.wait_ge(hid_used, b * C + 2 * C)
                    act.wait_ge(y_out, b * 16 + 16)
                    act.activation(v3(y_o, 2), v3(psum[:, 4 * BANK:6 * BANK], 2)[:, :, 0:D // 2],
                                   ACT.Copy).then_inc(y_cp, 1)
                    act.wait_ge(ht_ok, b + 2)
                    act.dma_start(xt, hs_dram[bass.ds(b * BR + 2 * BR, BR), :]).then_inc(xt_in, 16)
                    act.wait_ge(y_cp, b + 2)
                    act.dma_start(ys_dram[bass.ds(b * BR, BR), :], y_o).then_inc(y_out, 16)

            act.wait_ge(scattered, 16 * T)
            act.dma_start(xt, hs_dram[0:BR, :]).then_inc(xt_in, 16)

            def first_tokens(b):
                tokens_high(b)
                act.wait_ge(ht_ok, b + 1)
                act.dma_start(xt, hs_dram[BR:2 * BR, :]).then_inc(xt_in, 16)

            act.sem_inc(y_out, 16)
            expert_blocks(act, high_parts, first_tokens, block_steps)
            blocks = act.value_load(nblocks[0:1, 0:1], min_val=1, max_val=NB)
            act.wait_ge(xt_in, blocks * 16 + 32)
            act.wait_ge(y_out, blocks * 16 + 16)
            act.sem_inc(all_stored, 1)

        @block.vector
        def _(dve):
            n = [0]

            def link(ins):
                n[0] += 1
                ins.then_inc(step, 1)
                dve.wait_ge(step, n[0])

            last = [-1]

            def emptied_by(name, ins):
                assert plan[item[name]][1] == "D" and item[name] > last[0]
                last[0] = item[name]
                ins.then_inc(dve_emptied, 1)

            def variance(k, view, width):
                if k:
                    dve.wait_ge(rstd_ok, k)
                for t in range(T):
                    for q in range(2):
                        ins = dve.bn_stats(stats[:, t, 6 * q:6 * q + 6], view[:, t, q * width // 2:(q + 1) * width // 2])
                link(ins)
                for t in range(T):
                    ins = dve.bn_aggr(mv[:, t, :], stats[:, t, :])
                ins.then_inc(var_ok, 1)
                dve.wait_ge(rstd_ok, k + 1)

            def normal(out_, in_, t):
                return dve.tensor_scalar(out_, in_, mv[:, t, 0:1], rstd[:, t:t + 1], ALU.subtract, ALU.mult)

            dve.wait_ge(edges_in, 32)
            link(dve.tensor_copy(edge_f, edge_i))
            link(dve.tensor_reduce(mm_s[:, 0:1], edge_f[:, 1, :], AX_X, ALU.max))
            link(dve.tensor_reduce(mm_s[:, 1:2], edge_f[:, 1, :], AX_X, ALU.min))
            dve.wait_ge(consts, 1)
            for d in range(T):
                link(dve.tensor_scalar(h_a, mm_s[:, 0:1], float(P * d), None, ALU.is_ge))
                link(dve.tensor_scalar(h_b, mm_s[:, 1:2], float(P * d + P), None, ALU.is_lt))
                link(dve.tensor_tensor(h_a, h_a, h_b, ALU.mult))
                link(dve.tensor_scalar(v_b[:, 2 * d:2 * d + 2], g_i, h_a, None, ALU.mult))
            dve.sem_inc(bounds_v, 1)
            done(dve, ("edges",))
            dve.tensor_reduce(vm, place(("edges",))[0:2 * T, BANK:BANK + G], AX_X, ALU.max).then_inc(bounds_v, 1)
            emptied_by(("edges",), dve.tensor_copy(
                eT[:, :, :, 0:G], place(("edges",), 2 * J * G, P).rearrange("p (a j g) -> p a j g", a=2, j=J)))
            done(dve, ("bounds",))
            emptied_by(("bounds",), dve.tensor_copy(rr, place(("bounds",), 2 * T, 1)))
            was_emptied(dve, ("bounds",))
            rv = rr.rearrange("p (d a) -> p a d", a=2)
            link(dve.tensor_scalar(rv[:, 1, :], rv[:, 1, :], -1.0, float(G), ALU.mult, ALU.add))
            link(dve.tensor_scalar(rv[:, 1, :], rv[:, 1, :], float(G - 1), None, ALU.min))
            link(dve.tensor_tensor(rv[:, 0, :], rv[:, 0, :], rv[:, 1, :], ALU.subtract))
            link(dve.tensor_scalar(rv[:, 0, :], rv[:, 0, :], 1.0, None, ALU.max))
            dve.tensor_copy(ri, rr).then_inc(bounds_r, 1)

            dve.wait_ge(x_in, 16 * T)
            variance(0, tok, D)
            for t in range(T):
                normal(tok[:, t, :], tok[:, t, :], t).then_inc(ln_done["x0"], 1)
            for t in range(T):
                if plan[item["x0T", t]][1] == "D":
                    done(dve, ("x0T", t))
                    emptied_by(("x0T", t), dve.tensor_copy(aT6[:, :, t * P:(t + 1) * P], tview(("x0T", t), KD, P)))
            dve.wait_ge(arows1_in, 32)

            def attention_values(layer, t, heads, width, xl, rows):
                was_emptied(dve, (f"xl{layer}", t))
                for h in range(heads):
                    for q, (row, a) in enumerate(zip(rows, (a_src, a_dst))):
                        junk = TW + (2 * h + q) * width
                        ins = dve.tensor_tensor_reduce(low[0:P, junk:junk + width], xl[:, t, h * width:(h + 1) * width],
                                                       row[:, h * width:(h + 1) * width], 1.0, 0.0, ALU.mult,
                                                       ALU.add, a[:, t, h:h + 1])
                link(ins)

            for t in range(T):
                attention_values(1, t, HEADS, HID, xl1, row_a)
            dve.wait_ge(rows1_in, 64)
            for t in range(T):
                done(dve, ("res1", t))
                emptied_by(("res1", t), dve.tensor_tensor(res1[:, t, :], place(("res1", t), HC, P), row1["br1"], ALU.add))

            for d in range(T):
                lo = dve.value_load(ri[0:1, 2 * d + 1:2 * d + 2], min_val=0, max_val=G - 1)
                groups = dve.value_load(ri[0:1, 2 * d:2 * d + 1], min_val=1, max_val=G)
                with dve.Fori(0, groups) as i:
                    for j in range(J):
                        dve.wait_ge(oh_used[d], i * J + j + 1)
                        dve.tensor_scalar(oh_dst[:, j, :], iota16[:, P * d:P * d + P],
                                          eT[:, 1, j, bass.ds(lo + i, 1)], None, ALU.is_equal)
                        dve.tensor_scalar(oh_src[:, j, :], iota16[:, 0:N], eT[:, 0, j, bass.ds(lo + i, 1)], None,
                                          ALU.is_equal).then_inc(oh_ready[d], 1)
                done(dve, ("count", d))
                emptied_by(("count", d), dve.tensor_copy(counts[:, d, :], place(("count", d), N, P)))
                was_emptied(dve, ("count", d))
                diag = counts[:, d, P * d:P * d + P]
                link(dve.tensor_tensor(diag, diag, ident[0:P, 0:P], ALU.add))
                link(dve.tensor_scalar(absent[:, d, :], counts[:, d, :], 0.0, -BIG, ALU.is_equal, ALU.mult))

            diag_src = low[0:P, TW + XW + CWD:TW + XW + CWD + N]

            def source_diagonals(layer, h):
                if (layer, h) != (1, 0):
                    done(dve, ("src_row", *((layer, h - 1) if h else (1, HEADS - 1))))
                for t in range(T):
                    ins = dve.tensor_scalar(diag_src[:, t * P:(t + 1) * P], ident[0:P, 0:P], a_src[:, t, h:h + 1],
                                            None, ALU.mult)
                ins.then_inc(row_ok, 1)

            def graph_attention(layer, heads, width, agg, bias_row):
                n_, before_ = heads * T, 0 if layer == 1 else HEADS * T
                source_diagonals(layer, 0)
                for i in range(n_ + 3):
                    g = before_ + i
                    if i < n_:
                        dve.wait_ge(pair_ok, g + 1)
                        z = zbuf[g % 4]
                        link(dve.scalar_tensor_tensor(out=z, in0=z, scalar=0.2, in1=z, op0=ALU.mult, op1=ALU.max))
                        dve.tensor_tensor_reduce(z, z, absent[:, i % T, :], -1.0, 3e38, ALU.add, ALU.min,
                                                 negm[:, g % 4:g % 4 + 1]).then_inc(neg_ok, 1)
                        if i % T == 2 and i // T + 1 < heads:
                            source_diagonals(layer, i // T + 1)
                    if 1 <= i <= n_:
                        dve.wait_ge(exp_ok, g)
                        z, t = zbuf[(g - 1) % 4], (i - 1) % T
                        q = slice((g - 1) % 4, (g - 1) % 4 + 1)
                        dve.tensor_tensor_reduce(z, z, counts[:, t, :], 1.0, 0.0, ALU.mult, ALU.add,
                                                 rsum[:, q]).then_inc(prob_ok, 1)
                        dve.wait_ge(prob_ok, g)
                        link(dve.tensor_scalar(rsum[:, q], rsum[:, q], 1e-16, None, ALU.add))
                        link(dve.reciprocal(rinv[:, q], rsum[:, q]))
                    if i >= 3:
                        h, t = divmod(i - 3, T)
                        q = slice((g - 3) % 4, (g - 3) % 4 + 1)
                        done(dve, ("agg", layer, i - 3))
                        emptied_by(("agg", layer, i - 3), dve.scalar_tensor_tensor(
                            out=agg[:, t, h * width:(h + 1) * width], in0=place(("agg", layer, i - 3), width, P),
                            scalar=rinv[:, q], in1=bias_row[:, h * width:(h + 1) * width], op0=ALU.mult, op1=ALU.add))
                was_emptied(dve, ("agg", layer, n_ - 1))

            dve.wait_ge(padded, 32 * (D // 256))
            graph_attention(1, HEADS, HID, agg1, row1["b1"])
            variance(1, agg1, HC)
            for t in range(T):
                normal(agg1[:, t, :], agg1[:, t, :], t).then_inc(epi_a, 1)
            for t in range(T):
                dve.wait_ge(epi_b, t + 1)
                dve.scalar_tensor_tensor(out=res1[:, t, :], in0=agg1[:, t, :], scalar=0.0, in1=res1[:, t, :],
                                         op0=ALU.max, op1=ALU.add).then_inc(epi_c, 1)
            for t in range(T):
                if plan[item["h1T", t]][1] == "D":
                    done(dve, ("h1T", t))
                    emptied_by(("h1T", t), dve.tensor_copy(aT8[:, :, t * P:(t + 1) * P], tview(("h1T", t), KH, P)))
            dve.wait_ge(arows2_in, 32)
            for t in range(T):
                attention_values(2, t, 1, D, xl2, row_a2)
            dve.wait_ge(rows2_in, 64)
            for t in range(T):
                done(dve, ("res2", t))
                emptied_by(("res2", t), dve.tensor_tensor(res2[:, t, :], place(("res2", t), D, P), row2["br2"], ALU.add))
            graph_attention(2, 1, D, agg2, row2["b2"])
            variance(2, agg2, D)
            for t in range(T):
                normal(agg2[:, t, :], agg2[:, t, :], t).then_inc(epi_a, 1)
            dve.wait_ge(x2_in, 16)
            for t in range(T):
                dve.wait_ge(epi_b, T + t + 1)
                ins = dve.tensor_tensor(total[:, t, :], agg2[:, t, :], x_again[:, t, :], ALU.add)
            link(ins)
            variance(3, total, D)
            for t in range(T):
                ins = normal(tok[:, t, :], total[:, t, :], t)
            link(ins)
            variance(4, tok, D)
            for t in range(T):
                normal(agg2[:, t, :], tok[:, t, :], t).then_inc(ln_done["n1"], 1)
            dve.wait_ge(small_in, 80)

            def affine_T(name, t, dst, g):
                if plan[item[name, t]][1] == "D":
                    done(dve, (name, t))
                    for k in range(KD):
                        ins = dve.tensor_scalar(dst[:, k, t * P:(t + 1) * P], tview((name, t), KD, P)[:, k, :],
                                                cols[:, g, k:k + 1], cols[:, g + 1, k:k + 1], ALU.mult, ALU.add)
                    emptied_by((name, t), ins)

            for t in range(T):
                affine_T("hT", t, aT6, 0)
            for c in range(FC):
                done(dve, ("KT", c))
                emptied_by(("KT", c), dve.tensor_copy(KT[:, c, :], place(("KT", c), N)))
            dve.wait_ge(consts, 2)
            n_ = T * FH
            for i in range(n_ + 2):
                if i < n_:
                    w = (i // FH + 1) * P
                    done(dve, ("score", i))
                    if i >= 3:
                        done(dve, ("attT", i - 3))
                    emptied_by(("score", i), dve.tensor_tensor_reduce(
                        abuf[i % 3][:, 0:w], place(("score", i), w, P), causal[:, N - w:N], -SCALE, 3e38,
                        ALU.add, ALU.min, negm[:, i % 4:i % 4 + 1]))
                if i >= 2:
                    t, h = divmod(i - 2, FH)
                    q = slice((i - 2) % 4, (i - 2) % 4 + 1)
                    dve.wait_ge(sc_exp, i - 1)
                    link(dve.reciprocal(rinv[:, q], rsum[:, q]))
                    done(dve, ("pv", i - 2))
                    emptied_by(("pv", i - 2), dve.tensor_scalar(O[:, t, h * HS:(h + 1) * HS],
                                                                place(("pv", i - 2), HS, P), rinv[:, q], None, ALU.mult))
            for t in range(T):
                if plan[item["OT", t]][1] == "D":
                    done(dve, ("OT", t))
                    emptied_by(("OT", t), dve.tensor_copy(aT6[:, :, t * P:(t + 1) * P], tview(("OT", t), KD, P)))
            dve.wait_ge(late_in, 48)
            for t in range(T):
                done(dve, ("proj", t))
                emptied_by(("proj", t), dve.tensor_tensor(tok[:, t, :], place(("proj", t), D, P), tok[:, t, :], ALU.add))
                was_emptied(dve, ("proj", t))
                ins = dve.tensor_tensor(tok[:, t, :], tok[:, t, :], bp_row, ALU.add)
            link(ins)
            variance(5, tok, D)
            for t in range(T):
                normal(n2[:, t, :], tok[:, t, :], t).then_inc(ln_done["n2"], 1)
            for t in range(T):
                affine_T("h2T", t, h2T, 2)
            done(dve, ("gate",))
            emptied_by(("gate",), dve.tensor_copy(lg, v3(place(("gate",), T * E, P), T)))
            was_emptied(dve, ("gate",))
            def by_token(ap):
                return bass.AP(tensor=ap.tensor, offset=ap.offset, ap=[ap.ap[0], [1, T], [0, E]])
            link(dve.tensor_reduce(tmx, lg, AX_X, ALU.max))
            link(dve.tensor_tensor(sel, lg, by_token(tmx), ALU.is_equal))
            link(dve.tensor_tensor(sel, sel, spread(desc8, (P, T, E), 2), ALU.mult))
            link(dve.tensor_reduce(tmx, sel, AX_X, ALU.max))
            dve.tensor_tensor(sel, sel, by_token(tmx), ALU.is_equal).then_inc(sel_ok, 1)
            done(dve, ("rank",))
            emptied_by(("rank",), dve.tensor_copy(cum, v3(place(("rank",), (T + 1) * E, P), T + 1)))
            was_emptied(dve, ("rank",))
            number = cum[:, T, :]
            link(dve.tensor_scalar(nblk, number, 0.0, None, ALU.is_gt))
            for q in range(1, T):
                link(dve.scalar_tensor_tensor(out=nblk, in0=number, scalar=float(q * BR), in1=nblk,
                                              op0=ALU.is_gt, op1=ALU.add))
            link(dve.tensor_scalar(active, nblk, 0.0, None, ALU.is_gt))
            link(dve.tensor_tensor_scan(nblk_sum, nblk, zero8, 0.0, ALU.add, ALU.add))
            link(dve.tensor_tensor_scan(active_sum, active, zero8, 0.0, ALU.add, ALU.add))
            link(dve.tensor_tensor(start, nblk_sum, nblk, ALU.subtract))
            link(dve.tensor_tensor(order, active_sum, active, ALU.subtract))
            link(dve.tensor_scalar(base8, start, float(BR), None, ALU.mult))
            for t in range(T):
                link(dve.tensor_tensor(cum[:, t, :], cum[:, t, :], base8, ALU.add))
                link(dve.tensor_tensor_reduce(junk8, cum[:, t, :], sel[:, t, :], 1.0, 0.0, ALU.mult, ALU.add,
                                              pos_f[:, t:t + 1]))
            link(dve.tensor_copy(pos_i, pos_f))
            def over(ap, keep):
                return spread(ap, (1, NB, E), keep)
            link(dve.tensor_tensor(match, over(block_no, 1), over(start, 2), ALU.is_ge))
            link(dve.tensor_tensor(prod, over(block_no, 1), over(nblk_sum, 2), ALU.is_lt))
            link(dve.tensor_tensor(match, match, prod, ALU.mult))
            for q, what in enumerate((iota8, order)):
                link(dve.tensor_tensor(prod, match, over(what, 2), ALU.mult))
                link(dve.tensor_reduce(tab_f[:, q, :], prod, AX_X, ALU.add))
            link(dve.tensor_tensor(prod, over(block_no, 1), over(start, 2), ALU.is_equal))
            link(dve.tensor_tensor(prod, prod, match, ALU.mult))
            link(dve.tensor_reduce(tab_f[:, 2, :], prod, AX_X, ALU.add))
            link(dve.tensor_copy(tab_f[:, 3, NB - 1:NB], zero8[0:1, 0:1]))
            link(dve.tensor_copy(tab_f[:, 3, 0:NB - 1], tab_f[:, 2, 1:NB]))
            link(dve.tensor_copy(tab, tab_f))
            dve.tensor_copy(nblocks, nblk_sum[0:1, E - 1:E]).then_inc(routed, 1)
            done(dve, ("selT",))
            emptied_by(("selT",), dve.tensor_copy(v3(selT, T), tview(("selT",), T, P, E)))
            for t in range(T):
                done(dve, ("b2sum", t))
                emptied_by(("b2sum", t), dve.tensor_tensor(total[:, t, :], place(("b2sum", t), D, P), total[:, t, :], ALU.add))
                was_emptied(dve, ("b2sum", t))
                ins = dve.tensor_tensor(total[:, t, :], total[:, t, :], tok[:, t, :], ALU.add)
            link(ins)
            dve.sem_inc(final, 1)
            dve.sem_inc(hid_relu, 2)
            dve.sem_inc(low_ok, RING)

            def low_parts(a, b, w, c):
                for q in range(2):
                    u = unit_of[w, c, q]
                    dve.wait_ge(high_ok, a * U + (u + 1))
                    high_, low_ = unit_parts(u)
                    dve.tensor_tensor(low_, raw_view(u), high_, ALU.subtract).then_inc(low_ok, 1)

            def turn_in(b):
                dve.wait_ge(xt_used, b + 1)
                for k in range(KD):
                    ins = dve.tensor_scalar(turned[:, k, :], psum[:, 6 * BANK + k * BR:6 * BANK + (k + 1) * BR],
                                            cols[:, 2, k:k + 1], cols[:, 3, k:k + 1], ALU.mult, ALU.add)
                ins.then_inc(turned_ok, 1)

            def tokens_low(b):
                dve.wait_ge(hthi_ok, b + 1)
                dve.tensor_tensor(ht[1], turned, ht[0], ALU.subtract).then_inc(ht_ok, 1)

            def first_tokens(b):
                turn_in(b)
                tokens_low(b)

            def block_steps(b, e, s_):
                if s_ == 3:
                    turn_in(b + 1)
                if 1 <= s_ <= C:
                    c = s_ - 1
                    dve.wait_ge(hid_tr, b * C + (c + 3))
                    dve.wait_ge(hidhi_ok, b * C + (c + 1))
                    dve.wait_ge(hid_relu, b * C + (c + 2))
                    for j in range(CK):
                        ins = dve.tensor_scalar(
                            relu[:, j * BR:(j + 1) * BR], psum[:, (2 + c % 2) * BANK + j * BR:(2 + c % 2) * BANK + (j + 1) * BR],
                            b1T[:, bass.ds(e * (C * CK) + (c * CK + j), 1)], 0.0, ALU.add, ALU.max)
                    ins.then_inc(relu_ok, 1)
                    if c == C - 1:
                        tokens_low(b + 1)
                    dve.wait_ge(hidhi_ok, b * C + (c + 2))
                    dve.tensor_tensor(hidT[c % 2][1], v3(relu, CK), hidT[c % 2][0],
                                      ALU.subtract).then_inc(hid_relu, 1)

            dve.sem_inc(hidhi_ok, 1)
            expert_blocks(dve, low_parts, first_tokens, block_steps)
            for t in range(T):
                dve.wait_ge(gathered[t], 16)
                dve.tensor_tensor(total[:, t, :], total[:, t, :], back[t], ALU.add).then_inc(final, 1)

        @block.tensor
        def _(pe):
            def turn(name, k, tile):
                free(pe, name)
                w = tile.shape[-1] // k
                parts = tile.shape[0]
                for q in range(k):
                    ins = pe.transpose(place(name)[0:w, q * 128:q * 128 + parts], tile[:, q * w:(q + 1) * w],
                                       ident[0:parts, 0:parts])
                ins.then_inc(made, 1)

            def product(name, k, left, right, width, parts):
                free(pe, name)
                at = 0
                while at < width:
                    w = min(BANK, width - at)
                    for q in range(k):
                        ins = pe.matmul(place(name)[0:parts, at:at + w], left(q), right(q)[:, at:at + w],
                                        start=(q == 0), stop=(q == k - 1))
                    at += w
                ins.then_inc(made, 1)

            pe.wait_ge(bounds_v, 1)
            out_e = place(("edges",))
            for a in range(2):
                for j in range(J):
                    pe.transpose(out_e[0:P, (a * J + j) * G:(a * J + j + 1) * G], edge_f[:, a, P * j:P * j + P],
                                 ident[0:G, 0:G])
            pe.transpose(out_e[0:2 * T, BANK:BANK + G], v_b, ident[0:G, 0:G]).then_inc(made, 1)
            pe.wait_ge(bounds_v, 2)
            pe.transpose(place(("bounds",))[0:1, 0:2 * T], vm, ident[0:2 * T, 0:2 * T]).then_inc(made, 1)

            for t in range(T):
                pe.wait_ge(ln_done["x0"], t + 1)
                turn(("x0T", t), KD, tok[:, t, :])
            pe.wait_ge(w1g_in, 16)
            was_emptied(pe, ("x0T", T - 1))
            was_emptied(pe, ("x0T", T - 2))
            for t in range(T):
                product(("xl1", t), KD, lambda k: aT6[:, k, t * P:(t + 1) * P], lambda k: w1_g[:, k, :], HC, P)
            pe.wait_ge(wr1g_in, 16)
            for t in range(T):
                product(("res1", t), KD, lambda k: aT6[:, k, t * P:(t + 1) * P], lambda k: wr1_g[:, k, :], HC, P)
            pe.wait_ge(bounds_r, 1)
            for d in range(T):
                groups = pe.value_load(ri[0:1, 2 * d:2 * d + 1], min_val=1, max_val=G)
                free(pe, ("count", d))
                pe.sem_inc(oh_used[d], J)
                low_, high = place(("count", d))[0:P, 0:BANK], place(("count", d))[0:P, BANK:N]
                pe.matmul(low_, zero16[:, 0:P], zero16[:, 0:BANK], start=True, stop=False)
                pe.matmul(high, zero16[:, 0:P], zero16[:, 0:N - BANK], start=True, stop=False)
                with pe.Fori(0, groups) as i:
                    for j in range(J):
                        pe.wait_ge(oh_ready[d], i * J + j + 1)
                        pe.matmul(low_, oh_dst[:, j, :], oh_src[:, j, 0:BANK], start=False, stop=False)
                        pe.matmul(high, oh_dst[:, j, :], oh_src[:, j, BANK:N], start=False,
                                  stop=False).then_inc(oh_used[d], 1)
                pe.matmul(low_, zero16[:, 0:P], zero16[:, 0:BANK], start=False, stop=True)
                pe.matmul(high, zero16[:, 0:P], zero16[:, 0:N - BANK], start=False, stop=True).then_inc(made, 1)

            def graph_attention(layer, heads, width, xl):
                n_, before_ = heads * T, 0 if layer == 1 else HEADS * T
                for i in range(n_ + 2):
                    if i < n_ and i % T == 0:
                        name = ("src_row", layer, i // T)
                        free(pe, name)
                        pe.wait_ge(row_ok, i // T + 1 + (HEADS if layer == 2 else 0))
                        for c0, c1 in [(t * P, (t + 1) * P) for t in range(T - 1)] + [(N - P, BANK), (BANK, N)]:
                            ins = pe.matmul(place(name)[0:P, c0:c1], ones[0:P, 0:P],
                                            low[0:P, TW + XW + CWD + c0:TW + XW + CWD + c1], start=True, stop=True)
                        ins.then_inc(made, 1)
                    if 1 <= i <= n_:
                        pe.wait_ge(prob_ok, before_ + i)
                        turn(("probT", layer, i - 1), T, zbuf[(before_ + i - 1) % 4])
                    if i >= 2:
                        h = (i - 2) // T
                        was_emptied(pe, ("probT", layer, i - 2))
                        product(("agg", layer, i - 2), T, lambda k: probT[i % 2][:, k, :],
                                lambda k: xl[:, k, h * width:(h + 1) * width], width, P)

            graph_attention(1, HEADS, HID, xl1)
            for t in range(T):
                pe.wait_ge(epi_c, t + 1)
                turn(("h1T", t), KH, res1[:, t, :])
            pe.wait_ge(w2g_in, 16)
            was_emptied(pe, ("h1T", T - 1))
            was_emptied(pe, ("h1T", T - 2))
            for t in range(T):
                product(("xl2", t), KH, lambda k: aT8[:, k, t * P:(t + 1) * P], lambda k: w2_g[:, k, :], D, P)
            pe.wait_ge(wr2g_in, 16)
            for t in range(T):
                product(("res2", t), KH, lambda k: aT8[:, k, t * P:(t + 1) * P], lambda k: wr2_g[:, k, :], D, P)
            graph_attention(2, 1, D, xl2)
            for t in range(T):
                pe.wait_ge(ln_done["n1"], t + 1)
                turn(("hT", t), KD, agg2[:, t, :])
            pe.wait_ge(wq_in, 16 * KD)
            was_emptied(pe, ("hT", T - 1))
            was_emptied(pe, ("hT", T - 2))
            for c in range(FC):
                product(("QT", c), KD, lambda k: wq_s[:, k, c * 128:(c + 1) * 128], lambda k: aT6[:, k, :], N, 128)
            pe.wait_ge(wk_in, 16 * KD)
            for c in range(FC):
                product(("KT", c), KD, lambda k: wk_s[:, k, c * 128:(c + 1) * 128], lambda k: aT6[:, k, :], N, 128)
            pe.wait_ge(wv_in, 16 * KD)
            for t in range(T):
                product(("V", t), KD, lambda k: aT6[:, k, t * P:(t + 1) * P], lambda k: wv_s[:, k, :], D, P)
            was_emptied(pe, ("QT", FC - 1))
            was_emptied(pe, ("KT", FC - 1))
            n_ = T * FH
            for i in range(n_ + 2):
                if i < n_:
                    t, h = divmod(i, FH)
                    half_ = slice(64 * (h % 2), 64 * (h % 2) + 64)
                    product(("score", i), 1, lambda k: QT[half_, h // 2, t * P:(t + 1) * P],
                            lambda k: KT[half_, h // 2, :], (t + 1) * P, P)
                if 1 <= i <= n_:
                    t = (i - 1) // FH
                    pe.wait_ge(sc_exp, i)
                    turn(("attT", i - 1), t + 1, abuf[(i - 1) % 3][:, 0:(t + 1) * P])
                if i >= 2:
                    t, h = divmod(i - 2, FH)
                    if i == 2:
                        was_emptied(pe, ("V", T - 1))
                    was_emptied(pe, ("attT", i - 2))
                    product(("pv", i - 2), t + 1, lambda k: attT[i % 2][:, k, :],
                            lambda k: Vt[:, k, h * HS:(h + 1) * HS], HS, P)
            was_emptied(pe, ("pv", n_ - 1))
            for t in range(T):
                turn(("OT", t), KD, O[:, t, :])
            pe.wait_ge(wp_in, 16)
            was_emptied(pe, ("OT", T - 1))
            was_emptied(pe, ("OT", T - 2))
            for t in range(T):
                product(("proj", t), KD, lambda k: aT6[:, k, t * P:(t + 1) * P], lambda k: wp_s[:, k, :], D, P)
            pe.wait_ge(late_in, 48)
            turn(("b1T",), 2, b1_rows)
            for t in range(T):
                pe.wait_ge(ln_done["n2"], t + 1)
                turn(("h2T", t), KD, n2[:, t, :])
            pe.wait_ge(small_in, 80)
            was_emptied(pe, ("h2T", T - 1))
            was_emptied(pe, ("h2T", T - 2))
            free(pe, ("gate",))
            for t in range(T):
                for k in range(KD):
                    ins = pe.matmul(place(("gate",))[0:P, t * E:(t + 1) * E], h2T[:, k, t * P:(t + 1) * P],
                                    wg_s[:, k, :], start=(k == 0), stop=(k == KD - 1))
            ins.then_inc(made, 1)
            pe.wait_ge(sel_ok, 1)
            free(pe, ("rank",))
            for t in range(T + 1):
                for q in range(min(t + 1, T)):
                    ins = pe.matmul(place(("rank",))[0:P, t * E:(t + 1) * E],
                                    before if q == t else ones[0:P, 0:P], sel[:, q, :],
                                    start=(q == 0), stop=(q == min(t, T - 1)))
            ins.then_inc(made, 1)
            free(pe, ("selT",))
            for t in range(T):
                ins = pe.transpose(place(("selT",))[0:E, t * 128:t * 128 + P], sel[:, t, :], ident[0:P, 0:P])
            ins.then_inc(made, 1)
            was_emptied(pe, ("selT",))
            for t in range(T):
                product(("b2sum", t), 1, lambda k: selT[:, t * P:(t + 1) * P], lambda k: b2_s, D, P)
            was_emptied(pe, ("b2sum", T - 1))

            pe.wait_ge(routed, 1)
            blocks = pe.value_load(nblocks[0:1, 0:1], min_val=1, max_val=NB)
            pe.sem_inc(hid_tr, 2)
            pe.sem_inc(hid_mm, C)
            pe.sem_inc(hid_used, C)
            PARTS = ((0, 0), (0, 1), (1, 0))

            def turn_tokens(b):
                pe.wait_ge(xt_in, b * 16 + 16)
                for k in range(KD):
                    ins = pe.transpose(psum[:, 6 * BANK + k * BR:6 * BANK + (k + 1) * BR],
                                       xt[:, k * 128:(k + 1) * 128], ident)
                ins.then_inc(xt_used, 1)

            turn_tokens(0)
            with pe.Fori(0, blocks) as b:
                a = pe.value_load(tab[0:1, 1, bass.ds(b, 1)], min_val=0, max_val=E - 1)

                def first_product(c):
                    if c == 0:
                        pe.wait_ge(ht_ok, b + 1)
                    pe.wait_ge(low_ok, a * U + (RING + unit_of[1, c, 1] + 1))
                    pe.wait_ge(hid_cp, b * C + (c + 1))
                    for k in range(KD):
                        for x_, w_ in PARTS:
                            ins = pe.matmul(psum[:, (c % 2) * BANK:(c % 2 + 1) * BANK], ht[x_][:, k, :],
                                            w1_s[c][w_][:, k, :], start=(k == 0 and x_ + w_ == 0),
                                            stop=(k == KD - 1 and x_ == 1))
                    ins.then_inc(hid_mm, 1)

                def turn_hidden(c):
                    pe.wait_ge(hid_cp, b * C + (c + 3))
                    pe.wait_ge(hid_relu, b * C + (c + 1))
                    for j in range(CK):
                        ins = pe.transpose(psum[:, (2 + c % 2) * BANK + j * BR:(2 + c % 2) * BANK + (j + 1) * BR],
                                           hid[c % 2][:, j * 128:(j + 1) * 128], ident)
                    ins.then_inc(hid_tr, 1)

                def second_product(c):
                    pe.wait_ge(low_ok, a * U + (RING + unit_of[2, c, 1] + 1))
                    pe.wait_ge(hid_relu, b * C + (c + 3))
                    if c == 0:
                        pe.wait_ge(y_cp, b + 1)
                    for j in range(CK):
                        for x_, w_ in PARTS:
                            for q in range(2):
                                ins = pe.matmul(psum[:, (4 + q) * BANK:(4 + q) * BANK + D // 2],
                                                hidT[c % 2][x_][:, j, :],
                                                w2_s[c][w_][:, j, q * D // 2:(q + 1) * D // 2],
                                                start=(c == 0 and j == 0 and x_ + w_ == 0),
                                                stop=(c == C - 1 and j == CK - 1 and x_ == 1))
                    ins.then_inc(hid_used, 1)

                for s_ in range(C + 2):
                    if s_ < C:
                        first_product(s_)
                    if 1 <= s_ <= C:
                        turn_hidden(s_ - 1)
                    if s_ == 3:
                        turn_tokens(b + 1)
                    if s_ >= 2:
                        second_product(s_ - 2)


_INS = ['x', 'src', 'dst', 'L0_gnn_W1', 'L0_gnn_a_src1', 'L0_gnn_a_dst1', 'L0_gnn_b1', 'L0_gnn_g1', 'L0_gnn_be1',
        'L0_gnn_Wr1', 'L0_gnn_br1', 'L0_gnn_W2', 'L0_gnn_a_src2', 'L0_gnn_a_dst2', 'L0_gnn_b2', 'L0_gnn_g2',
        'L0_gnn_be2', 'L0_gnn_Wr2', 'L0_gnn_br2', 'L0_ffn_ln1_g', 'L0_ffn_ln1_b', 'L0_ffn_ln2_g', 'L0_ffn_ln2_b',
        'L0_ffn_Wq', 'L0_ffn_Wk', 'L0_ffn_Wv', 'L0_ffn_Wp', 'L0_ffn_bp', 'L0_ffn_Wg', 'L0_ffn_W1', 'L0_ffn_b1',
        'L0_ffn_W2', 'L0_ffn_b2']
_OUTS = [((625, 768), 'float32')]


def kernel(**inputs):
    import numpy as _np
    import concourse.bacc as _bacc
    from concourse import mybir as _mybir
    from concourse.bass_utils import run_bass_kernel_spmd as _run

    nc = _bacc.Bacc("TRN2", target_bir_lowering=False, num_devices=1)
    arrays, args = {}, []
    for name in _INS:
        a = _np.ascontiguousarray(inputs[name])
        arrays[f"in_{name}_dram"] = a
        args.append(nc.dram_tensor(f"in_{name}_dram", a.shape, _mybir.dt.from_np(a.dtype), kind="ExternalInput").ap())
    for i, (shape, dtype) in enumerate(_OUTS):
        dt = _mybir.dt.from_np(_np.dtype(dtype))
        args.append(nc.dram_tensor(f"out_{i}_dram", shape, dt, kind="ExternalOutput").ap())
    gnn_moe_kernel(nc, *args)
    r = _run(nc, [arrays], core_ids=[0])
    got = tuple(r.results[0][f"out_{i}_dram"] for i in range(len(_OUTS)))
    return got[0]
```
